# Optimizing a Trainium2 kernel written in Bass

```python
import numpy as np
import jax
import jax.numpy as jnp

def _softmax(x, axis=-1):
    return jax.nn.softmax(x, axis=axis)

def _gelu(x):
    return jax.nn.gelu(x, approximate=True)

def _silu(x):
    return jax.nn.silu(x)

def _sigmoid(x):
    return jax.nn.sigmoid(x)

def _layernorm(x, axis=-1, eps=1e-05):
    m = jnp.mean(x, axis=axis, keepdims=True)
    v = jnp.var(x, axis=axis, keepdims=True)
    return (x - m) / jnp.sqrt(v + eps)

def _scatter_add(tgt, idx, src, axis=0):
    return tgt.at[idx].add(src)

def _segment_sum(src, seg, n):
    return jax.ops.segment_sum(src, seg, n)
kernel_name = 'mk_vit_tower_postln_d1_tok_img256_r4_62a9c7'

def setup_inputs(seed: int=0):
    np.random.seed(seed)
    _w = jnp.asarray

    def _rec_inputs():
        import jax
        import jax.numpy as jnp
        _rk = jax.random.key(seed)
        x = -0.00040386 + 0.999972 * jax.random.normal(jax.random.fold_in(_rk, 1), (4, 3, 224, 224), jnp.float32)
        return x
    x = _rec_inputs()

    def _L0_tok_setup():
        import jax, jax.numpy as jnp
        import numpy as np
        EPS = 1e-05
        P = 8
        DIM = 64
        NUM_TOKENS = 64
        PATCH_DIM = 3 * P * P

        def layernorm(x, g, b):
            mu = jnp.mean(x, axis=-1, keepdims=True)
            var = jnp.mean(jnp.square(x - mu), axis=-1, keepdims=True)
            return (x - mu) * jax.lax.rsqrt(var + EPS) * g + b
        key = jax.random.key(seed)
        ks = jax.random.split(key, 8)
        b, c, h, w = (16, 3, 128, 128)
        x = jax.random.normal(ks[0], (b, c, h, w), dtype=jnp.float32)
        ln1_g = jnp.ones((PATCH_DIM,), jnp.float32)
        ln1_b = jnp.zeros((PATCH_DIM,), jnp.float32)
        W1 = jax.random.normal(ks[1], (PATCH_DIM, DIM), jnp.float32) * 0.02
        b1 = jnp.zeros((DIM,), jnp.float32)
        ln2_g = jnp.ones((DIM,), jnp.float32)
        ln2_b = jnp.zeros((DIM,), jnp.float32)
        Wp1 = jax.random.normal(ks[2], (DIM, DIM), jnp.float32) * 0.02
        bp1 = jnp.zeros((DIM,), jnp.float32)
        lnp_g = jnp.ones((DIM,), jnp.float32)
        lnp_b = jnp.zeros((DIM,), jnp.float32)
        Wp2 = jax.random.normal(ks[3], (DIM, NUM_TOKENS), jnp.float32) * 0.02
        bp2 = jnp.zeros((NUM_TOKENS,), jnp.float32)
        return {'x': x, 'ln1_g': ln1_g, 'ln1_b': ln1_b, 'W1': W1, 'b1': b1, 'ln2_g': ln2_g, 'ln2_b': ln2_b, 'Wp1': Wp1, 'bp1': bp1, 'lnp_g': lnp_g, 'lnp_b': lnp_b, 'Wp2': Wp2, 'bp2': bp2}
    _L0_tok_all = _L0_tok_setup()
    _L0_tok_in = {k: v for k, v in _L0_tok_all.items() if k in ('ln1_g', 'ln1_b', 'W1', 'b1', 'ln2_g', 'ln2_b', 'Wp1', 'bp1', 'lnp_g', 'lnp_b', 'Wp2', 'bp2')}
    del _L0_tok_all

    def _L0_attn_setup():
        import jax, jax.numpy as jnp
        import numpy as np
        TEMPERATURE = 1.0
        W_BLEND = 0.8
        EPS = 1e-12

        def _l2norm(x):
            n = jnp.sqrt(jnp.sum(x * x, axis=-1, keepdims=True))
            return x / jnp.maximum(n, EPS)
        key = jax.random.key(seed)
        feats = jax.random.normal(key, (4, 512, 64), dtype=jnp.float32)
        return {'feats': feats}
    _L0_attn_all = _L0_attn_setup()
    _L0_attn_in = {k: v for k, v in _L0_attn_all.items() if k in ()}
    del _L0_attn_all

    def _L0_ffn_setup():
        import math
        import jax, jax.numpy as jnp
        import numpy as np
        CAPACITY_FACTOR = 1.25
        key = jax.random.key(seed)
        ks = jax.random.split(key, 5)
        B, L, D, F, E = (8, 2048, 64, 256, 8)
        h = jax.random.normal(ks[0], (B, L, D), dtype=jnp.float32)
        gate_w = jax.random.normal(ks[1], (D, E), dtype=jnp.float32) * 0.02
        gate_b = jnp.zeros((E,), dtype=jnp.float32)
        w1 = jax.random.normal(ks[2], (E, D, F), dtype=jnp.float32) * (1.0 / math.sqrt(D))
        b1 = jnp.zeros((E, F), dtype=jnp.float32)
        w2 = jax.random.normal(ks[3], (E, F, D), dtype=jnp.float32) * (1.0 / math.sqrt(F))
        b2 = jnp.zeros((E, D), dtype=jnp.float32)
        return {'h': h, 'gate_w': gate_w, 'gate_b': gate_b, 'w1': w1, 'b1': b1, 'w2': w2, 'b2': b2}
    _L0_ffn_all = _L0_ffn_setup()
    _L0_ffn_in = {k: v for k, v in _L0_ffn_all.items() if k in ('gate_w', 'gate_b', 'w1', 'b1', 'w2', 'b2')}
    del _L0_ffn_all
    return {'x': x, 'L0_tok_ln1_g': _L0_tok_in['ln1_g'], 'L0_tok_ln1_b': _L0_tok_in['ln1_b'], 'L0_tok_W1': _L0_tok_in['W1'], 'L0_tok_b1': _L0_tok_in['b1'], 'L0_tok_ln2_g': _L0_tok_in['ln2_g'], 'L0_tok_ln2_b': _L0_tok_in['ln2_b'], 'L0_tok_Wp1': _L0_tok_in['Wp1'], 'L0_tok_bp1': _L0_tok_in['bp1'], 'L0_tok_lnp_g': _L0_tok_in['lnp_g'], 'L0_tok_lnp_b': _L0_tok_in['lnp_b'], 'L0_tok_Wp2': _L0_tok_in['Wp2'], 'L0_tok_bp2': _L0_tok_in['bp2'], 'L0_ffn_gate_w': _L0_ffn_in['gate_w'], 'L0_ffn_gate_b': _L0_ffn_in['gate_b'], 'L0_ffn_w1': _L0_ffn_in['w1'], 'L0_ffn_b1': _L0_ffn_in['b1'], 'L0_ffn_w2': _L0_ffn_in['w2'], 'L0_ffn_b2': _L0_ffn_in['b2']}

def reference(x, L0_tok_ln1_g, L0_tok_ln1_b, L0_tok_W1, L0_tok_b1, L0_tok_ln2_g, L0_tok_ln2_b, L0_tok_Wp1, L0_tok_bp1, L0_tok_lnp_g, L0_tok_lnp_b, L0_tok_Wp2, L0_tok_bp2, L0_ffn_gate_w, L0_ffn_gate_b, L0_ffn_w1, L0_ffn_b1, L0_ffn_w2, L0_ffn_b2):
    import jax
    import jax.numpy as jnp

    def _L0_tok_ref(x, ln1_g, ln1_b, W1, b1, ln2_g, ln2_b, Wp1, bp1, lnp_g, lnp_b, Wp2, bp2):
        import jax, jax.numpy as jnp
        import numpy as np
        EPS = 1e-05
        P = 8
        DIM = 64
        NUM_TOKENS = 64
        PATCH_DIM = 3 * P * P

        def layernorm(x, g, b):
            mu = jnp.mean(x, axis=-1, keepdims=True)
            var = jnp.mean(jnp.square(x - mu), axis=-1, keepdims=True)
            return (x - mu) * jax.lax.rsqrt(var + EPS) * g + b
        b, c, H, W = x.shape
        hp, wp = (H // P, W // P)
        patches = x.reshape(b, c, hp, P, wp, P)
        patches = jnp.transpose(patches, (0, 2, 4, 3, 5, 1))
        patches = patches.reshape(b, hp * wp, P * P * c)
        tokens = layernorm(patches, ln1_g, ln1_b)
        tokens = tokens @ W1 + b1
        tokens = layernorm(tokens, ln2_g, ln2_b)
        q = tokens
        k = tokens
        tokens = jnp.concatenate([q, k, tokens], axis=1)
        h1 = layernorm(tokens @ Wp1 + bp1, lnp_g, lnp_b)
        h1 = jax.nn.silu(h1)
        return h1 @ Wp2 + bp2

    def _L0_attn_ref(feats):
        import jax, jax.numpy as jnp
        import numpy as np
        TEMPERATURE = 1.0
        W_BLEND = 0.8
        EPS = 1e-12

        def _l2norm(x):
            n = jnp.sqrt(jnp.sum(x * x, axis=-1, keepdims=True))
            return x / jnp.maximum(n, EPS)
        B, N, C = feats.shape
        f = _l2norm(feats.reshape(B * N, C))
        scores = jnp.matmul(f, f.T) / TEMPERATURE
        attn = jax.nn.softmax(scores, axis=-1)
        feats_att = jnp.matmul(attn, f)
        feats_fcm = f * W_BLEND + feats_att * (1.0 - W_BLEND)
        return _l2norm(feats_fcm.reshape(B, N, C))

    def _L0_ffn_ref(h, gate_w, gate_b, w1, b1, w2, b2):
        import math
        import jax, jax.numpy as jnp
        import numpy as np
        CAPACITY_FACTOR = 1.25
        B, L, D = h.shape
        E = gate_w.shape[1]
        T = B * L
        C = max(1, math.ceil(CAPACITY_FACTOR * T / E))
        x = h.reshape(T, D)
        logits = x @ gate_w + gate_b
        probs = jax.nn.softmax(logits, axis=-1)
        idx = jnp.argmax(probs, axis=-1)
        prb = jnp.take_along_axis(probs, idx[:, None], axis=1)[:, 0]
        one_hot = jax.nn.one_hot(idx, E, dtype=jnp.float32)
        pos = (jnp.cumsum(one_hot, axis=0) * one_hot).sum(-1).astype(jnp.int32) - 1
        kept = pos < C
        pos_safe = jnp.where(kept, pos, C)
        buf = jnp.zeros((E, C, D), dtype=h.dtype).at[idx, pos_safe].set(x, mode='drop')
        hmid = jax.nn.relu(jnp.einsum('ecd,edf->ecf', buf, w1) + b1[:, None, :])
        ybuf = jnp.einsum('ecf,efd->ecd', hmid, w2) + b2[:, None, :]
        pos_g = jnp.minimum(pos, C - 1)
        y_tok = ybuf[idx, pos_g] * (prb * kept)[:, None]
        y = y_tok.reshape(B, L, D)
        y = jnp.nan_to_num(y, nan=0.0, posinf=10000.0, neginf=-10000.0)
        return y
    h = _L0_tok_ref(x, L0_tok_ln1_g, L0_tok_ln1_b, L0_tok_W1, L0_tok_b1, L0_tok_ln2_g, L0_tok_ln2_b, L0_tok_Wp1, L0_tok_bp1, L0_tok_lnp_g, L0_tok_lnp_b, L0_tok_Wp2, L0_tok_bp2)
    h = _layernorm(h + _L0_attn_ref(h), axis=-1)
    h = _layernorm(h + _L0_ffn_ref(h, L0_ffn_gate_w, L0_ffn_gate_b, L0_ffn_w1, L0_ffn_b1, L0_ffn_w2, L0_ffn_b2), axis=-1)
    return h

_drawn_inputs = setup_inputs


def setup_inputs(seed=0):
    import zlib

    import numpy as np

    out = dict(_drawn_inputs(seed))
    spreads = {'L0_tok_ln1_g': (1.0, 0.2),
     'L0_tok_ln1_b': (0.0, 0.1),
     'L0_tok_b1': (0.0, 0.1),
     'L0_tok_ln2_g': (1.0, 0.2),
     'L0_tok_ln2_b': (0.0, 0.1),
     'L0_tok_bp1': (0.0, 0.1),
     'L0_tok_lnp_g': (1.0, 0.2),
     'L0_tok_lnp_b': (0.0, 0.1),
     'L0_tok_bp2': (0.0, 0.1),
     'L0_ffn_gate_b': (0.0, 0.1),
     'L0_ffn_b1': (0.0, 0.8),
     'L0_ffn_b2': (0.0, 0.652)}
    factors = {}
    for name, (base, spread) in spreads.items():
        noise = np.random.default_rng([zlib.crc32(name.encode()), seed]).standard_normal(out[name].shape)
        drawn = base * np.exp(spread * noise) if base else spread * noise
        out[name] = jnp.asarray(drawn.astype(out[name].dtype))
    for name, factor in factors.items():
        out[name] = (out[name] * factor).astype(out[name].dtype)
    return out
```

```python
from contextlib import ExitStack

import numpy as np

import concourse.bass as bass
from concourse import mybir

F32 = mybir.dt.float32
F16 = mybir.dt.float16
U32 = mybir.dt.uint32
I32 = mybir.dt.int32
ACT = mybir.ActivationFunctionType
ALU = mybir.AluOpType
AX = mybir.AxisListType

B, CH, IMG, PATCH = 4, 3, 224, 8
HP = IMG // PATCH
ROWS = B * HP
W = HP
D = 64
D2 = 2 * D
PD = CH * PATCH * PATCH
HALF = PD // 2
GW = 4
NB = W // GW
BLK = GW * ROWS
T = ROWS * W
COPIES = 3
E = 8
F = 256
FC = F // 128
CAP = -(-5 * COPIES * T // (4 * E))
KT_FULL = T // 128
KT_REST = T - KT_FULL * 128
KT = KT_FULL + 1
NPAIR = KT_FULL // 2 + 1
LAST = NPAIR - 1
LASTW = (NB - 1) * GW
EPS = 1e-5
NORM_EPS = 1e-12
BIG = 3.4028234663852886e38
INF_AS = 10000.0
SPLIT = 256.0
WTOP = 8192.0
C_IDENT, C_STACK, C_BASE, C_IMAGE, C_RAMP = 0, 128, 192, 192 + ROWS, 192 + 2 * ROWS
C_COLS = C_RAMP + E


def shape_constants():
    c = np.zeros((128, C_COLS), np.float32)
    c[:, C_IDENT:C_IDENT + 128] = np.eye(128)
    c[:, C_STACK:C_STACK + D] = np.tile(np.eye(D), (2, 1))
    b, hp = np.divmod(np.arange(ROWS), HP)
    before = COPIES * (b[:, None] < b[None, :]) + (b[:, None] == b[None, :]) * (hp[:, None] < hp[None, :])
    c[:ROWS, C_BASE:C_BASE + ROWS] = before
    c[:ROWS, C_IMAGE:C_IMAGE + ROWS] = b[:, None] == b[None, :]
    c[:, C_RAMP:C_RAMP + E] = E - np.arange(E)
    return c


def add(n, k):
    return n + k if k else n


def vit_layer(nc, consts, x, ln1_g, ln1_b, W1, b1, ln2_g, ln2_b, Wp1, bp1, lnp_g, lnp_b, Wp2, bp2,
              gate_w, gate_b, w1, eb1, w2, eb2, out):
    with ExitStack() as ctx:
        def sb(name, shape, dt=F32):
            return ctx.enter_context(nc.sbuf_tensor(name, shape, dt))

        def sem(name):
            return ctx.enter_context(nc.semaphore(name))

        cst = sb("cst", [128, C_COLS])
        ident = cst[:, C_IDENT:C_IDENT + 128]
        img = sb("img", [ROWS, CH * PATCH, W, PATCH])
        xn = sb("xn", [ROWS, W, PD])
        xt = sb("xt", [HALF, 2, 2, BLK])
        stats = sb("stats", [ROWS, W, 6])
        ones_col = sb("ones_col", [128, 1])
        half_neg = sb("half_neg", [ROWS, W])
        w1t = sb("w1t", [HALF, 2, D])
        g1c = sb("g1c", [HALF, 2, 1])
        bl1c = sb("bl1c", [HALF, 2, 1])
        bl1b = sb("bl1b", [HALF, 2, ROWS])
        w1g = sb("w1g", [HALF, 2, D])
        wp1 = sb("wp1", [D, D])
        g2c = sb("g2c", [D2, 1])
        bl2c = sb("bl2c", [D, 1])
        bl2b = sb("bl2b", [D, ROWS])
        wp1d = sb("wp1d", [D2, 2, D])
        wp1s = sb("wp1s", [D2, D])
        wp2d = sb("wp2d", [D2, 2, D])
        rowsb = sb("rowsb", [128, 5, D])
        gbias = sb("gbias", [128, E])
        bias1 = sb("bias1", [ROWS, D])
        bias2 = sb("bias2", [ROWS, D])
        cen = sb("cen", [128, 8])
        gwz = sb("gwz", [D2, E])
        ew1 = sb("ew1", [128, E, F])
        ew1s = sb("ew1s", [128, E, F])
        ew1h = sb("ew1h", [128, E, F], F16)
        ew1l = sb("ew1l", [128, E, F], F16)
        ew2 = sb("ew2", [128, E * FC, D])
        eb1r = sb("eb1r", [E * FC, 128])
        eb1s = sb("eb1s", [128, E * FC])
        b2d = sb("b2d", [GW * E, GW, D])
        wmax = sb("wmax", [128, 8])
        room = sb("room", [ROWS, 3 * W * D])

        def part(at, *shape):
            n, axes = 1, " ".join(f"a{i}" for i in range(len(shape)))
            for k in shape:
                n *= k
            return room[:, at:at + n].rearrange(f"p ({axes}) -> p {axes}", **{f"a{i}": k for i, k in enumerate(shape)})

        ta, tb, tc = (part(k * W * D, W, D) for k in range(3))
        cols = sb("cols", [D2, 2, 2 * ROWS])
        h_all = sb("h_all", [ROWS, W, D])
        f_all = sb("f_all", [ROWS, W, D])
        fdup = img[:].rearrange("p q w r -> p (q w r)")[:, 0:W * 2 * D].rearrange("p (w a d) -> p w a d", a=2, d=D)
        small = sb("small", [ROWS, 12, W])
        fT = xn[0:D].rearrange("p w f -> p (w f)")[:, 0:T]
        QH = sb("QH", [128, T], F16)
        QL = sb("QL", [128, T], F16)
        KHL = sb("KHL", [128, KT * 128], F16)
        f2 = sb("f2", [128, KT_FULL + 1, D])
        NE = 3
        ex = sb("ex", [128, NE, 2, BLK])
        esum = sb("esum", [128, 2, BLK])
        att = sb("att", [128, BLK])
        h2dup = sb("h2dup", [ROWS, GW, 2, D])
        xcol = sb("xcol", [128, BLK])
        xhl = sb("xhl", [128, 2, BLK], F16)
        lg = sb("lg", [ROWS, 4, GW, E])
        lgo = sb("lgo", [ROWS, GW, E])
        ones_run = sb("ones_run", [ROWS, E * W])
        ps_small = sb("ps_small", [ROWS, 12, GW])
        ohT = sb("ohT", [GW * E, ROWS])
        oh_all = sb("oh_all", [ROWS, W, E])
        ohs_all = sb("ohs_all", [ROWS, W, E])
        yb_all = sb("yb_all", [ROWS, W, D])
        h2_all = sb("h2_all", [ROWS, W, D])
        hm = ew1s[:].rearrange("p e f -> p (e f)")[:, 0:4 * BLK].rearrange("p (n t) -> p n t", n=4)
        yt = part(0, 4, GW, 2, D)
        ya = part(8 * GW * D, 6, GW, D)
        pt = part(14 * GW * D, 4, GW, D)
        rest = part(18 * GW * D, 3, GW, D)
        zeros = sb("zeros", [ROWS, GW, D])
        mask = sb("mask", [ROWS, GW, D], I32)
        fin_small = sb("fin_small", [ROWS, 8, GW])
        fin_t = sb("fin_t", [ROWS, 4, GW, D])
        outcomes = img[:].rearrange("p q w r -> p (q w r)").rearrange("p (k w d) -> p k w d", k=3, d=D)
        ok_all, od_all = outcomes[:, 0], outcomes[:, 1]
        ohe = sb("ohe", [ROWS, E, W])
        pre = sb("pre", [ROWS, E, W])
        rk = sb("rk", [ROWS, 3, W, E])
        rk_small = sb("rk_small", [ROWS, 4, E])
        kept = sb("kept", [ROWS, COPIES, W])
        rkw = sb("rkw", [ROWS, 3, W])
        o_all = xn[:].rearrange("p w f -> p (w f)").rearrange("p (c w d) -> p c w d", c=COPIES, d=D)

        pS = ctx.enter_context(nc.psum_tensor("pS", [128, 4, 512], F32))
        pR = ctx.enter_context(nc.psum_tensor("pR", [128, 4, 512], F32))
        pAV = pR[:, 0, 0:BLK]
        pY = [pR[0:ROWS, 1 + i, :].rearrange("p (w e d) -> p w e d", w=GW, e=2) for i in range(2)]
        pM = pR[:, 3, :]
        pA = pM[0:ROWS, 0:GW * D].rearrange("p (w d) -> p w d", d=D)
        pDen = pM[0:ROWS, GW * D:GW * D + GW]
        pLog = pM[0:ROWS, 0:GW * E].rearrange("p (w e) -> p w e", e=E)

        def pT(g):
            return pR[0:ROWS, g % 4, 0:GW * D].rearrange("p (w d) -> p w d", d=D)

        ld_img, ld_cst, ld_w1, ld_tok, ld_rows, ld_exp, ld_exp2 = (
            sem(n) for n in ("ld_img", "ld_cst", "ld_w1", "ld_tok", "ld_rows", "ld_exp", "ld_exp2"))
        zeroed = sem("zeroed")
        dv = sem("dv")
        dvp = sem("dvp")
        dvf = sem("dvf")
        s_root_in, s_root = sem("s_root_in"), sem("s_root")
        s_proot_in, s_proot = sem("s_proot_in"), sem("s_proot")
        s_froot_in, s_froot = sem("s_froot_in"), sem("s_froot")
        s_wts = sem("s_wts")
        s_bias = sem("s_bias")
        s_biasc = sem("s_biasc")
        s_wmax_in, s_wmax = sem("s_wmax_in"), sem("s_wmax")
        s_wscale = sem("s_wscale")
        s_wcut = sem("s_wcut")
        s_xn = sem("s_xn")
        s_tr = sem("s_tr")
        s_trc = sem("s_trc")
        s_mm = sem("s_mm")
        s_ev = sem("s_ev")
        s_sq = sem("s_sq")
        s_act = sem("s_act")
        s_fd = sem("s_fd")
        s_ft = sem("s_ft")
        s_ftc = sem("s_ftc")
        s_ql = sem("s_ql")
        s_khl = sem("s_khl")
        s_f2 = sem("s_f2")
        s_f2c = sem("s_f2c")
        s_S = sem("s_S")
        s_exp = sem("s_exp")
        s_es = sem("s_es")
        s_av = sem("s_av")
        s_att = sem("s_att")
        s_pnum = sem("s_pnum")
        s_h2 = sem("s_h2")
        s_h2t = sem("s_h2t")
        s_xc = sem("s_xc")
        s_x16 = sem("s_x16")
        s_log = sem("s_log")
        s_lm = sem("s_lm")
        s_pe = sem("s_pe")
        s_ohp = sem("s_ohp")
        s_oht = sem("s_oht")
        s_ohtc = sem("s_ohtc")
        s_yb = sem("s_yb")
        s_route = sem("s_route")
        s_l1 = sem("s_l1")
        s_relu = sem("s_relu")
        s_l2 = sem("s_l2")
        s_part = sem("s_part")
        s_ysum = sem("s_ysum")
        pls = sem("pls")
        s_cnt_in, s_cnt = sem("s_cnt_in"), sem("s_cnt")
        s_out = sem("s_out")
        st_out = sem("st_out")

        ctx.enter_context(nc.allow_non_contiguous_dma(reason="a few hundred gains and biases, one to a partition"))
        block = ctx.enter_context(nc.Block())

        img_src = x.rearrange("b c (h q) w -> b h c (q w)", q=PATCH)

        def load_image(eng, b):
            for c in range(CH):
                dst = img[b * HP:(b + 1) * HP, c * PATCH:(c + 1) * PATCH].rearrange("p q w r -> p (q w r)")
                eng.dma_start(dst, img_src[b, :, c]).then_inc(ld_img, 16)

        @block.sync
        def _(sp):
            for b in (0, 1, 2, 3):
                load_image(sp, b)
            sp.dma_start(cst[:], consts).then_inc(ld_cst, 16)
            sp.dma_start(ew1[0:D], w1.rearrange("e d f -> d e f")).then_inc(ld_exp, 16)
            sp.dma_start(ew1[D:D2], w1.rearrange("e d f -> d e f")).then_inc(ld_exp, 16)
            sp.dma_start(ew2[:], w2.rearrange("e (c p) d -> p (e c) d", p=128)).then_inc(ld_exp2, 16)
            sp.dma_start(eb1r[:], eb1.rearrange("e (c p) -> (e c) p", p=128)).then_inc(ld_exp2, 16)
            for n, (w0, w1_) in enumerate(((0, LASTW), (LASTW, W))):
                for c in range(COPIES):
                    sp.wait_ge(s_out, n * COPIES + c + 1)
                    for b in range(B):
                        dst = out[b].rearrange("(c h w) d -> c h (w d)", c=COPIES, h=HP)[c]
                        src = o_all[b * HP:(b + 1) * HP, c, w0:w1_].rearrange("p w d -> p (w d)")
                        sp.dma_start(dst[:, w0 * D:w1_ * D], src).then_inc(st_out, 16)
            sp.wait_ge(st_out, 2 * 16 * COPIES * B)

        @block.gpsimd
        def _(pool):
            def row(v, n):
                return v.rearrange("(a n) -> a n", a=1).broadcast_to([128, n])

            w1v = W1.rearrange("(q c) d -> c q d", c=CH)
            g1v = ln1_g.rearrange("(q c a) -> c q a", c=CH, a=1)
            b1v = ln1_b.rearrange("(q c a) -> c q a", c=CH, a=1)
            for dst, src in ((w1t, w1v), (g1c, g1v), (bl1c, b1v)):
                pool.dma_start(dst[0:64, 0], src[0]).then_inc(ld_w1, 16)
                pool.dma_start(dst[64:96, 0], src[1, 0:32]).then_inc(ld_w1, 16)
                pool.dma_start(dst[0:32, 1], src[1, 32:64]).then_inc(ld_w1, 16)
                pool.dma_start(dst[32:96, 1], src[2]).then_inc(ld_w1, 16)
            for n, v in enumerate((b1, bp1, lnp_g, lnp_b, bp2)):
                pool.dma_start(rowsb[:, n], row(v, D)).then_inc(ld_rows, 16)
            pool.dma_start(gbias[:], row(gate_b, E)).then_inc(ld_rows, 16)
            nc.gpsimd.memset(half_neg[:], -0.5).then_inc(zeroed, 1)
            nc.gpsimd.memset(ones_col[:], 1.0).then_inc(zeroed, 1)
            nc.gpsimd.memset(wp1d[:], 0.0).then_inc(zeroed, 1)
            nc.gpsimd.memset(wp2d[:], 0.0).then_inc(zeroed, 1)
            nc.gpsimd.memset(gwz[:], 0.0).then_inc(zeroed, 1)
            nc.gpsimd.memset(b2d[:], 0.0).then_inc(zeroed, 1)
            nc.gpsimd.memset(KHL[:, T:KT * 128], 0.0).then_inc(zeroed, 1)
            pool.wait_ge(zeroed, 7)
            nc.gpsimd.memset(f2[KT_REST:128, KT_FULL], 0.0).then_inc(zeroed, 1)
            pool.wait_ge(zeroed, 8)
            nc.gpsimd.memset(zeros[:], 0.0).then_inc(zeroed, 1)
            pool.wait_ge(zeroed, 9)
            pool.dma_start(wp1[:], Wp1).then_inc(ld_tok, 16)
            pool.dma_start(wp1s[0:D], Wp1).then_inc(ld_tok, 16)
            pool.dma_start(wp1s[D:D2], Wp1).then_inc(ld_tok, 16)
            for half in range(2):
                pool.dma_start(g2c[half * D:(half + 1) * D], ln2_g.rearrange("(n a) -> n a", a=1)).then_inc(ld_tok, 16)
                pool.dma_start(wp2d[half * D:(half + 1) * D, half], Wp2).then_inc(ld_tok, 16)
            pool.dma_start(bl2c[:], ln2_b.rearrange("(n a) -> n a", a=1)).then_inc(ld_tok, 16)
            pool.dma_start(gwz[0:D], gate_w).then_inc(ld_tok, 16)
            for w in range(GW):
                pool.dma_start(b2d[w * E:(w + 1) * E, w], eb2).then_inc(ld_tok, 16)

            for n in range(4):
                pool.wait_ge(s_root_in, n + 1)
                nc.gpsimd.tensor_tensor(small[:, 2 * n + 1], small[:, 2 * n], half_neg[:], ALU.pow).then_inc(s_root, 1)
                if n == 0:
                    pool.wait_ge(s_wmax_in, 1)
                    nc.gpsimd.partition_all_reduce(wmax[:, 1:2], wmax[:, 0:1], 128,
                                                   bass.bass_isa.ReduceOp.max).then_inc(s_wmax, 1)

            pool.wait_ge(s_wscale, 1)
            nc.gpsimd.tensor_scalar(ew1s[:], ew1[:], wmax[:, 4:5], None, ALU.mult).then_inc(s_wcut, 1)
            pool.wait_ge(s_wcut, 1)
            nc.gpsimd.tensor_copy(ew1h[:], ew1s[:]).then_inc(s_wcut, 1)
            pool.wait_ge(s_wcut, 2)
            nc.gpsimd.tensor_tensor(ew1l[:], ew1s[:], ew1h[:], ALU.subtract).then_inc(s_wcut, 1)

            def roots(n, src, dst, sin, sout):
                pool.wait_ge(sin, add(n, 1))
                nc.gpsimd.tensor_tensor(dst, src, half_neg[:, 0:GW], ALU.pow).then_inc(sout, 1)

            def post(j):
                roots(2 * j, ps_small[:, 1], ps_small[:, 2], s_proot_in, s_proot)
                roots(2 * j + 1, ps_small[:, 4], ps_small[:, 5], s_proot_in, s_proot)

            def experts(j):
                base = j * 13
                for p in range(4):
                    pool.wait_ge(s_part, add(j * 4, p + 3))
                    nc.gpsimd.tensor_tensor(ya[:, p], yt[:, p, :, 0], yt[:, p, :, 1], ALU.add).then_inc(pls, 1)
                    if p:
                        pool.wait_ge(pls, add(base, 2 * p))
                        first = ya[:, 0] if p == 1 else ya[:, 4]
                        nc.gpsimd.tensor_tensor(ya[:, 4], first, ya[:, p], ALU.add).then_inc(pls, 1)
                pool.wait_ge(pls, add(base, 7))
                nc.gpsimd.tensor_tensor(ya[:, 5], ya[:, 4], yb_all[:, bass.ds(j * GW, GW)], ALU.add).then_inc(pls, 1)
                y = ya[:, 5]
                pool.wait_ge(pls, add(base, 8))
                nc.gpsimd.tensor_tensor(ya[:, 0], y, zeros[:], ALU.mult).then_inc(pls, 1)
                nc.gpsimd.tensor_scalar(rest[:, 0], y, BIG, INF_AS, ALU.is_gt, ALU.mult).then_inc(pls, 1)
                nc.gpsimd.tensor_scalar(rest[:, 1], y, -BIG, -INF_AS, ALU.is_lt, ALU.mult).then_inc(pls, 1)
                pool.wait_ge(pls, add(base, 11))
                nc.gpsimd.tensor_tensor(rest[:, 0], rest[:, 0], rest[:, 1], ALU.add).then_inc(pls, 1)
                nc.gpsimd.tensor_scalar(mask[:], ya[:, 0], 0.0, -1.0, ALU.is_equal, ALU.mult).then_inc(pls, 1)
                pool.wait_ge(pls, add(base, 13))
                nc.gpsimd.tensor_tensor(rest[:, 2], rest[:, 0], h2_all[:, bass.ds(j * GW, GW)], ALU.add).then_inc(s_ysum, 1)
                roots(2 * j, fin_small[:, 1], fin_small[:, 2], s_froot_in, s_froot)
                roots(2 * j + 1, fin_small[:, 4], fin_small[:, 5], s_froot_in, s_froot)

            with pool.Fori(1, NB - 1) as j:
                post(j - 1)
                experts(j - 1)
            post(NB - 2)
            post(NB - 1)
            experts(NB - 2)
            experts(NB - 1)

        @block.scalar
        def _(act):
            for g in range(NB):
                act.wait_ge(s_tr, g + 1)
                if g >= 2:
                    act.wait_ge(s_mm, g - 1)
                nc.scalar.copy(xt[:, g % 2], pS[0:HALF, 2 * (g % 2):2 * (g % 2) + 2, 0:BLK]).then_inc(s_trc, 1)
            def copy_cols(n0, groups):
                for g in groups:
                    act.wait_ge(s_tr, n0 + g + 1)
                    act.wait_ge(s_mm, n0 + max(g - 1, 0))
                    nc.scalar.copy(cols[:, g % 2], pS[0:D2, g % 4, 0:2 * ROWS]).then_inc(s_trc, 1)

            def squares(n, src, dst):
                act.wait_ge(s_ev, n)
                nc.scalar.square(dst, src).then_inc(s_sq, 1)

            copy_cols(NB, range(4))
            squares(NB, ta[:], tb[:])
            copy_cols(NB, range(4, NB))
            squares(2 * NB, ta[:], tb[:])
            act.wait_ge(s_act, 1)
            nc.scalar.activation(tb[:], tc[:], ACT.Tanh, scale=0.5).then_inc(s_sq, 1)
            copy_cols(2 * NB, range(NB))
            squares(3 * NB, h_all[:], tb[:])
            for g in range(NB):
                act.wait_ge(s_ft, g + 1)
                nc.scalar.copy(QH[:, g * BLK:(g + 1) * BLK], pS[:, g % 4, 0:BLK]).then_inc(s_ftc, 1)
                nc.scalar.copy(fT[:, g * BLK:(g + 1) * BLK], pS[0:D, g % 4, 0:BLK]).then_inc(s_ftc, 1)
            for g in range(4):
                act.wait_ge(s_f2, g + 1)
                n = 8 if g < 3 else 1
                m = 128 if g < 3 else KT_REST
                nc.scalar.copy(f2[0:m, 8 * g:8 * g + n], pR[0:m, g, 0:n * D].rearrange("p (n d) -> p n d", d=D)).then_inc(s_f2c, 1)

            def exponentials(j, first, lone=False):
                for p in range(NPAIR):
                    act.wait_ge(s_S, add(j * NPAIR, p + 1))
                    if not (first and p < NE):
                        act.wait_ge(s_av, add(j * NPAIR, max(p + 1 - NE, 0)))
                        act.wait_ge(s_es, add(j * NPAIR, max(p + 1 - NE, 0)))
                    if p < LAST:
                        o, i = ex[:, p % NE], pS[:, 2 * (p % 2):2 * (p % 2) + 2, 0:BLK]
                    else:
                        o, i = ex[:, p % NE, 0], pS[:, 2 * (p % 2), 0:BLK]
                    nc.scalar.activation(o, i, ACT.Exp, scale=1.0 / (SPLIT * SPLIT)).then_inc(s_exp, 1)
                    if p == 9 and not first:
                        gate_exp(j - 1)
                act.wait_ge(s_av, add(j * NPAIR, NPAIR))
                if not first:
                    act.wait_ge(s_pnum, j)
                nc.scalar.copy(att[:], pAV).then_inc(s_att, 1)

            def gate_exp(j):
                act.wait_ge(s_lm, add(j, 1))
                nc.scalar.activation(lg[:, 3], lg[:, 2], ACT.Exp).then_inc(s_pe, 1)

            def relus(j, next_gate=None):
                for c in range(E * FC):
                    act.wait_ge(s_l1, add(j * E * FC, c + 1))
                    act.wait_ge(s_l2, add(j * E, c // FC + 1))
                    nc.scalar.activation(hm[:, c % 4], pS[:, c % 4, 0:BLK], ACT.Relu, bias=eb1s[:, c:c + 1]).then_inc(s_relu, 1)
                    if next_gate is not None and c == 11:
                        gate_exp(next_gate)

            act.wait_ge(s_wscale, 1)
            exponentials(0, True)
            with act.Fori(1, NB - 1) as j:
                exponentials(j, False)
                relus(j - 1)
            exponentials(NB - 1, False)
            relus(NB - 2, NB - 1)
            relus(NB - 1)

        @block.tensor
        def _(pe):
            MM = pe.matmul
            pe.sem_inc(s_l2, 2)
            pe.wait_ge(ld_cst, 16)
            pe.wait_ge(s_wts, 1)
            for c in range(2):
                MM(pR[0:ROWS, 3, 0:D], bl1b[:, c], w1t[:, c], start=(c == 0), stop=(c == 1))
            MM(pR[0:ROWS, 3, D:D2], bl2b[:], wp1[:], start=True, stop=True)
            pe.wait_ge(ld_exp2, 32)
            pe.transpose(pR[:, 3, 128:128 + E * FC], eb1r[:], ident[0:E * FC, 0:E * FC]).then_inc(s_bias, 1)

            def tokenize(g):
                pe.wait_ge(s_xn, g + 1)
                if g >= 2:
                    pe.wait_ge(s_trc, g - 1)
                for w in range(GW):
                    for c in range(2):
                        i = pe.transpose(pS[0:HALF, 2 * (g % 2) + c, w * ROWS:(w + 1) * ROWS],
                                         xn[:, g * GW + w, c * HALF:(c + 1) * HALF], ident[0:ROWS, 0:ROWS])
                i.then_inc(s_tr, 1)

            def project(g):
                pe.wait_ge(s_trc, g + 1)
                if g == 3:
                    pe.wait_ge(s_biasc, 1)
                if g >= 4:
                    pe.wait_ge(s_ev, g - 3)
                for w in range(GW):
                    for c in range(2):
                        i = MM(pT(g)[:, w], xt[:, g % 2, c, w * ROWS:(w + 1) * ROWS], w1g[:, c],
                               start=(c == 0), stop=(c == 1))
                i.then_inc(s_mm, 1)

            for g in range(NB + 1):
                if g < NB:
                    tokenize(g)
                if g:
                    project(g - 1)

            def layer(n, src, weights, ready, count):
                for g in range(NB + 1):
                    if g < NB:
                        pe.wait_ge(ready, count(g))
                        if g >= 4:
                            pe.wait_ge(s_trc, n * NB + g - 3)
                        elif n:
                            pe.wait_ge(s_trc, n * NB)
                        for q in range(2):
                            w = g * GW + 2 * q
                            i = pe.transpose(pS[0:D2, g % 4, q * ROWS:(q + 1) * ROWS],
                                             src[:, w:w + 2].rearrange("p w d -> p (w d)"), ident[0:ROWS, 0:ROWS])
                        i.then_inc(s_tr, 1)
                    if g:
                        pe.wait_ge(s_trc, n * NB + g)
                        pe.wait_ge(s_ev, n * NB + max(g - 4, 0))
                        for q in range(2):
                            i = MM(pT(g - 1)[:, 2 * q:2 * q + 2].rearrange("p w d -> p (w d)"),
                                   cols[:, (g - 1) % 2, q * ROWS:(q + 1) * ROWS],
                                   weights[:].rearrange("p w d -> p (w d)"), start=True, stop=True)
                        i.then_inc(s_mm, 1)

            layer(1, ta, wp1d, s_ev, lambda g: g + 1)
            layer(2, tc, wp2d, s_act, lambda g: g + 2)

            for g in range(NB):
                pe.wait_ge(s_fd, 1)
                if g >= 4:
                    pe.wait_ge(s_ftc, 2 * (g - 3))
                    pe.wait_ge(s_ql, g - 3)
                for w in range(GW):
                    i = pe.transpose(pS[:, g % 4, w * ROWS:(w + 1) * ROWS],
                                     fdup[:, g * GW + w].rearrange("p a d -> p (a d)"), ident[0:ROWS, 0:ROWS])
                i.then_inc(s_ft, 1)
            pe.wait_ge(s_ftc, 2 * NB)
            pe.wait_ge(s_ev, 3 * NB)
            for k in range(KT_FULL + 1):
                m = 128 if k < KT_FULL else KT_REST
                i = pe.transpose(pR[0:m, k // 8, (k % 8) * D:(k % 8 + 1) * D], fT[:, k * 128:k * 128 + m],
                                 ident[0:D, 0:D])
                if k % 8 == 7 or k == KT_FULL:
                    i.then_inc(s_f2, 1)

            def scores(j, first, p):
                if p < 2:
                    if not first:
                        pe.wait_ge(s_exp, j * NPAIR)
                else:
                    pe.wait_ge(s_exp, add(j * NPAIR, p - 1))
                tiles = 2 if p < LAST else 1
                for t in range(tiles):
                    k0 = (2 * p + t) * 128
                    o = pS[:, 2 * (p % 2) + t, 0:BLK]
                    MM(o, KHL[:, k0:k0 + 128], QH[:, bass.ds(j * BLK, BLK)], start=True, stop=False)
                    i = MM(o, KHL[:, k0:k0 + 128], QL[:, bass.ds(j * BLK, BLK)], start=False, stop=True)
                i.then_inc(s_S, 1)

            def values(j, first, p):
                pe.wait_ge(s_exp, add(j * NPAIR, p + 1))
                if p == 0 and not first:
                    pe.wait_ge(s_att, j)
                if p < LAST:
                    for t in range(2):
                        i = MM(pR[t * D:(t + 1) * D, 0, 0:BLK], f2[:, 2 * p + t], ex[:, p % NE, t],
                               start=(p == 0), stop=(p == LAST - t))
                else:
                    i = MM(pR[0:D, 0, 0:BLK], f2[:, 2 * p], ex[:, p % NE, 0],
                           start=False, stop=True)
                i.then_inc(s_av, 1)

            def post_sums(j):
                pe.wait_ge(s_es, add(j * NPAIR, NPAIR))
                pe.wait_ge(s_att, add(j, 1))
                if isinstance(j, int):
                    pe.wait_ge(s_route, j)
                for w in range(GW):
                    q = slice(w * ROWS, (w + 1) * ROWS)
                    for t in range(2):
                        MM(pDen[:, w:w + 1], esum[:, t, q], ones_col[:], start=(t == 0), stop=(t == 1))
                for w in range(GW):
                    q = slice(w * ROWS, (w + 1) * ROWS)
                    i = MM(pA[:, w], att[:, q], cst[:, C_STACK:C_STACK + D], start=True, stop=True)
                i.then_inc(s_pnum, 1)

            def post_cols(j):
                pe.wait_ge(s_h2, add(j, 1))
                for w in range(GW):
                    i = pe.transpose(pM[:, w * ROWS:(w + 1) * ROWS], h2dup[:, w].rearrange("p a d -> p (a d)"),
                                     ident[0:ROWS, 0:ROWS])
                i.then_inc(s_h2t, 1)

            def post_gate(j):
                pe.wait_ge(s_x16, add(j, 1))
                for w in range(GW):
                    i = MM(pLog[:, w], xcol[:, w * ROWS:(w + 1) * ROWS], gwz[:], start=True, stop=True)
                i.then_inc(s_log, 1)

            def post_turn(j):
                pe.wait_ge(s_ohp, add(j, 1))
                pe.transpose(pM[0:GW * E, 0:ROWS], lgo[:].rearrange("p w e -> p (w e)"),
                             ident[0:ROWS, 0:ROWS]).then_inc(s_oht, 1)

            def post_b2(j):
                pe.wait_ge(s_ohtc, add(j, 1))
                MM(pA.rearrange("p w d -> p (w d)"), ohT[:], b2d[:].rearrange("p w d -> p (w d)"),
                   start=True, stop=True).then_inc(s_yb, 1)

            def attention(j, first):
                for p in range(NPAIR + 1):
                    if p < NPAIR:
                        scores(j, first, p)
                    if p:
                        values(j, first, p - 1)
                    if not first:
                        if p == 0:
                            post_sums(j - 1)
                        if p == 6:
                            post_cols(j - 1)
                        if p == 8:
                            post_gate(j - 1)
                        if p == 11:
                            post_turn(j - 1)
                        if p == 12:
                            post_b2(j - 1)

            def hidden(j, c, slot):
                if c >= 4:
                    pe.wait_ge(s_relu, add(j * E * FC, c - 3))
                o = pS[:, c % 4, 0:BLK]
                e, k = c // FC, (c % FC) * 128
                MM(o, ew1h[:, e, k:k + 128], xhl[:, slot], start=True, stop=False)
                MM(o, ew1l[:, e, k:k + 128], xhl[:, slot], start=False, stop=True).then_inc(s_l1, 1)

            def outputs(j, e):
                pe.wait_ge(s_relu, add(j * E * FC, FC * e + FC))
                if e % 2 == 0:
                    pe.wait_ge(s_part, add(j * 4, e // 2 + 1))
                for w in range(GW):
                    for c in range(FC):
                        i = MM(pY[(e // 2) % 2][:, w, e % 2], hm[:, (FC * e + c) % 4, w * ROWS:(w + 1) * ROWS],
                               ew2[:, FC * e + c], start=(c == 0), stop=(c == FC - 1))
                i.then_inc(s_l2, 1)

            def queue_bases():
                pe.wait_ge(s_cnt_in, 1)
                MM(pM[0:ROWS, 0:E], cst[0:ROWS, C_BASE:C_BASE + ROWS], rk_small[:, 0], start=True, stop=True)
                MM(pM[0:ROWS, E:2 * E], cst[0:ROWS, C_IMAGE:C_IMAGE + ROWS], rk_small[:, 0],
                   start=True, stop=True).then_inc(s_cnt, 1)

            def experts(j, last_post=False, slot=0):
                j_is_last = slot == 1
                pe.wait_ge(s_exp, NPAIR * NB if j_is_last else add(j * NPAIR, 2 * NPAIR))
                if j_is_last:
                    pe.wait_ge(s_relu, j * E * FC)
                pe.wait_ge(s_x16, add(j, 1))
                for e in range(E + 1):
                    if e < E:
                        for c in range(FC):
                            hidden(j, FC * e + c, slot)
                    if e:
                        outputs(j, e - 1)
                    if last_post:
                        if e == 0:
                            post_sums(NB - 1)
                        if e == 4:
                            post_cols(NB - 1)
                        if e == 5:
                            post_gate(NB - 1)
                        if e == 7:
                            post_turn(NB - 1)
                        if e == 8:
                            post_b2(NB - 1)
                    if j_is_last and e == 1:
                        queue_bases()

            pe.wait_ge(s_khl, 2)
            pe.wait_ge(zeroed, 8)
            pe.wait_ge(s_f2c, 4)
            attention(0, True)
            pe.wait_ge(s_wcut, 3)
            with pe.Fori(1, NB - 1) as j:
                attention(j, False)
                experts(j - 1)
            attention(NB - 1, False)
            experts(NB - 2, last_post=True)
            experts(NB - 1, slot=1)

        @block.vector
        def _(dve):
            V = nc.vector

            class Steps:

                def __init__(self, s, base=0):
                    self.s, self.base, self.n = s, base, 0

                def __call__(self, ins):
                    self.n += 1
                    ins.then_inc(self.s, 1)
                    dve.wait_ge(self.s, add(self.base, self.n))

            step = Steps(dv)

            def bc(ap, n=D):
                return ap.unsqueeze(ap.ndim).broadcast_to([*ap.shape, n])

            def rows(v, n):
                return v.unsqueeze(1).broadcast_to([ROWS, n, v.shape[-1]])

            dve.sem_inc(s_part, 2)
            dve.wait_ge(ld_cst, 16)

            dve.wait_ge(ld_w1, 12 * 16)
            dve.wait_ge(zeroed, 8)
            dve.wait_ge(ld_tok, (9 + GW) * 16)
            dve.wait_ge(ld_rows, 6 * 16)
            step(V.memset(bl1b[:], 1.0))
            step(V.memset(bl2b[:], 1.0))
            for c in range(2):
                step(V.tensor_scalar(bl1b[:, c], bl1b[:, c], bl1c[:, c], None, ALU.mult))
                step(V.tensor_scalar(w1g[:, c], w1t[:, c], g1c[:, c], None, ALU.mult))
            step(V.tensor_scalar(bl2b[:], bl2b[:], bl2c[:], None, ALU.mult))
            step(V.tensor_reduce(cen[0:HALF, 0:2], w1g[:], AX.X, ALU.add))
            step(V.tensor_scalar(cen[0:HALF, 2:4], cen[0:HALF, 0:2], 1.0 / D, None, ALU.mult))
            for c in range(2):
                step(V.tensor_scalar(w1g[:, c], w1g[:, c], cen[0:HALF, 2 + c:3 + c], None, ALU.subtract))
            step(V.tensor_scalar(wp1s[:], wp1s[:], g2c[:], None, ALU.mult))
            step(V.tensor_reduce(cen[:, 4:5], wp1s[:], AX.X, ALU.add))
            step(V.tensor_scalar(cen[:, 5:6], cen[:, 4:5], 1.0 / D, None, ALU.mult))
            for half in range(2):
                r = slice(half * D, (half + 1) * D)
                step(V.tensor_scalar(wp1d[r, half], wp1s[r], cen[r, 5:6], None, ALU.subtract))
                step(V.tensor_scalar(wp2d[r, half], wp2d[r, half], 0.5, None, ALU.mult))
            dve.sem_inc(s_wts, 1)

            dve.wait_ge(ld_img, CH * B * 16)
            for w in range(W):
                i = V.bn_stats(stats[:, w], img[:, :, w, :])
            step(i)
            me, mo, ve, vo = (stats[:, :, k] for k in (1, 4, 2, 5))
            dif, dif2, vsum = small[:, 8], small[:, 9], small[:, 10]
            step(V.tensor_tensor(dif, me, mo, ALU.subtract))
            step(V.tensor_tensor(small[:, 11], me, mo, ALU.add))
            step(V.tensor_tensor(dif2, dif, dif, ALU.mult))
            step(V.tensor_tensor(vsum, ve, vo, ALU.add))
            step(V.tensor_scalar(dif2, dif2, 0.25, EPS, ALU.mult, ALU.add))
            step(V.scalar_tensor_tensor(small[:, 0], vsum, 1.0 / PD, dif2, ALU.mult, ALU.add))
            step(V.tensor_scalar(small[:, 8], small[:, 11], 0.5, None, ALU.mult))
            dve.sem_inc(s_root_in, 1)
            dve.wait_ge(s_bias, 1)
            for n, (dst, k) in enumerate(((bias1, 0), (bias2, 1))):
                step(V.tensor_tensor(dst[:], pR[0:ROWS, 3, n * D:(n + 1) * D], rowsb[0:ROWS, k], ALU.add))
                step(V.tensor_reduce(cen[0:ROWS, 6:7], dst[:], AX.X, ALU.add))
                step(V.tensor_scalar(cen[0:ROWS, 7:8], cen[0:ROWS, 6:7], 1.0 / D, None, ALU.mult))
                step(V.tensor_scalar(dst[:], dst[:], cen[0:ROWS, 7:8], None, ALU.subtract))
            step(V.tensor_copy(eb1s[:], pR[:, 3, 128:128 + E * FC]))
            dve.sem_inc(s_biasc, 1)
            dve.wait_ge(s_root, 1)
            for w in range(W):
                i = V.tensor_scalar(xn[:, w].rearrange("p (a r) -> p a r", r=PATCH), img[:, :, w, :],
                                    small[:, 8, w:w + 1], small[:, 1, w:w + 1], ALU.subtract, ALU.mult)
                if w % GW == GW - 1:
                    i.then_inc(s_xn, 1)

            def root(n, ssq, scale, eps):
                step(V.tensor_scalar(small[:, 2 * n], ssq, scale, eps, ALU.mult, ALU.add))
                dve.sem_inc(s_root_in, 1)
                dve.wait_ge(s_root, n + 1)

            dve.wait_ge(ld_exp, 32)
            V.tensor_reduce(wmax[:, 0:1], ew1[:].rearrange("p e f -> p (e f)"), AX.X, ALU.max,
                            apply_absolute_value=True).then_inc(s_wmax_in, 1)

            for g in range(NB):
                dve.wait_ge(s_mm, g + 1)
                V.tensor_tensor(ta[:, g * GW:(g + 1) * GW], pT(g), rows(bias1[:], GW), ALU.add).then_inc(s_ev, 1)
            dve.wait_ge(s_sq, 1)
            step(V.tensor_reduce(small[:, 9], tb[:], AX.X, ALU.add))
            root(1, small[:, 9], 1.0 / D, EPS)
            dve.wait_ge(s_wmax, 1)
            step(V.tensor_scalar(wmax[:, 2:3], wmax[:, 1:2], 1e-30, None, ALU.max))
            step(V.tensor_scalar(wmax[:, 3:4].bitcast(I32), wmax[:, 2:3].bitcast(I32), 0x7F800000, None,
                                 ALU.bitwise_and))
            step(V.reciprocal(wmax[:, 5:6], wmax[:, 3:4]))
            step(V.tensor_scalar(wmax[:, 4:5], wmax[:, 5:6], WTOP, None, ALU.mult))
            step(V.tensor_scalar(wmax[:, 6:7], wmax[:, 3:4], 1.0 / (WTOP * SPLIT), None, ALU.mult))
            step(V.tensor_scalar(eb1s[:], eb1s[:], wmax[:, 4:5], SPLIT, ALU.mult, ALU.mult))
            dve.sem_inc(s_wscale, 1)
            for g in range(NB):
                r = small[:, 3, g * GW:(g + 1) * GW]
                dve.wait_ge(s_mm, NB + g + 1)
                step(V.tensor_tensor(tc[:, g * GW:(g + 1) * GW], pT(g), bc(r), ALU.mult))
                V.tensor_tensor(ta[:, g * GW:(g + 1) * GW], tc[:, g * GW:(g + 1) * GW], rows(bias2[:], GW),
                                ALU.add).then_inc(s_ev, 1)
            dve.wait_ge(s_sq, 2)
            step(V.tensor_reduce(small[:, 9], tb[:], AX.X, ALU.add))
            root(2, small[:, 9], 1.0 / D, EPS)
            step(V.tensor_tensor(tc[:], ta[:], bc(small[:, 5]), ALU.mult))
            step(V.tensor_tensor(ta[:], tc[:], rows(rowsb[0:ROWS, 2], W), ALU.mult))
            V.tensor_tensor(tc[:], ta[:], rows(rowsb[0:ROWS, 3], W), ALU.add).then_inc(s_act, 1)
            dve.wait_ge(s_act, 1)
            dve.wait_ge(s_sq, 3)
            for g in range(NB):
                q = slice(g * GW, (g + 1) * GW)
                V.scalar_tensor_tensor(tc[:, q], tb[:, q], 1.0, tc[:, q], ALU.add, ALU.mult).then_inc(s_act, 1)
            for g in range(NB):
                dve.wait_ge(s_mm, 2 * NB + g + 1)
                V.tensor_tensor(h_all[:, g * GW:(g + 1) * GW], pT(g), rows(rowsb[0:ROWS, 4], GW), ALU.add).then_inc(s_ev, 1)
            dve.wait_ge(s_sq, 4)
            step(V.tensor_reduce(small[:, 9], tb[:], AX.X, ALU.add))
            root(3, small[:, 9], 1.0, 0.0)
            step(V.tensor_scalar(small[:, 10], small[:, 7], 1.0 / NORM_EPS, SPLIT, ALU.min, ALU.mult))
            dve.wait_ge(s_ev, 3 * NB)
            step(V.tensor_tensor(f_all[:], h_all[:], bc(small[:, 10]), ALU.mult))
            step(V.tensor_copy(fdup[:, :, 0], f_all[:]))
            V.tensor_copy(fdup[:, :, 1], f_all[:]).then_inc(s_fd, 1)
            for g in range(NB):
                q = slice(g * BLK, (g + 1) * BLK)
                dve.wait_ge(s_ftc, 2 * (g + 1))
                V.tensor_tensor(QL[:, q], pS[:, g % 4, 0:BLK], QH[:, q], ALU.subtract).then_inc(s_ql, 1)
            dve.wait_ge(s_ql, NB)
            V.tensor_copy(KHL[0:D, 0:T], QH[0:D]).then_inc(s_khl, 1)
            V.tensor_copy(KHL[D:D2, 0:T], QL[D:D2]).then_inc(s_khl, 1)

            NPOST = 29

            def post_steps(j, at):
                s = Steps(dvp, j * NPOST)
                s.n = at
                return s

            def post_norm(j, s):
                blk = bass.ds(j * GW, GW)
                dve.wait_ge(s_pnum, add(j, 1))
                s(V.reciprocal(ps_small[:, 0], pDen))
                s(V.tensor_scalar(ps_small[:, 0], ps_small[:, 0], 0.2, None, ALU.mult))
                s(V.tensor_tensor(pt[:, 0], pA, bc(ps_small[:, 0]), ALU.mult))
                s(V.scalar_tensor_tensor(pt[:, 1], f_all[:, blk], 0.8, pt[:, 0], ALU.mult, ALU.add))
                s(V.tensor_tensor(pt[:, 2], pt[:, 1], pt[:, 1], ALU.mult))
                V.tensor_reduce(ps_small[:, 1], pt[:, 2], AX.X, ALU.add).then_inc(s_proot_in, 1)

            def post_center(j, s):
                blk = bass.ds(j * GW, GW)
                dve.wait_ge(s_proot, add(j * 2, 1))
                s(V.tensor_scalar(ps_small[:, 3], ps_small[:, 2], 1.0 / (NORM_EPS * SPLIT), None, ALU.min))
                s(V.tensor_tensor(pt[:, 0], pt[:, 1], bc(ps_small[:, 3]), ALU.mult))
                s(V.tensor_tensor(pt[:, 1], pt[:, 0], h_all[:, blk], ALU.add))
                s(V.tensor_reduce(ps_small[:, 6], pt[:, 1], AX.X, ALU.add))
                s(V.scalar_tensor_tensor(pt[:, 2], bc(ps_small[:, 6]), -1.0 / D, pt[:, 1], ALU.mult, ALU.add))
                s(V.tensor_tensor(pt[:, 3], pt[:, 2], pt[:, 2], ALU.mult))
                s(V.tensor_reduce(ps_small[:, 7], pt[:, 3], AX.X, ALU.add))
                V.tensor_scalar(ps_small[:, 4], ps_small[:, 7], 1.0 / D, EPS, ALU.mult, ALU.add).then_inc(s_proot_in, 1)

            def post_h2(j, s):
                dve.wait_ge(s_proot, add(j * 2, 2))
                s(V.tensor_tensor(h2dup[:, :, 0], pt[:, 2], bc(ps_small[:, 5]), ALU.mult))
                s(V.tensor_copy(h2dup[:, :, 1], h2dup[:, :, 0]))
                dve.sem_inc(s_h2, 1)
                s(V.tensor_copy(h2_all[:, bass.ds(j * GW, GW)], h2dup[:, :, 0]))

            def post_split(j, s, slot):
                dve.wait_ge(s_h2t, add(j, 1))
                s(V.tensor_copy(xcol[:], pM[:, 0:BLK]))
                s(V.tensor_scalar(xhl[:, slot], xcol[:], SPLIT, None, ALU.mult))
                s(V.scalar_tensor_tensor(xhl[D:D2, slot], xcol[D:D2], SPLIT, xhl[D:D2, slot],
                                         ALU.mult, ALU.subtract))
                dve.sem_inc(s_x16, 1)

            def post_route(j, s):
                blk = bass.ds(j * GW, GW)
                dve.wait_ge(s_log, add(j, 1))
                s(V.tensor_tensor(lg[:, 0], pLog, rows(gbias[0:ROWS], GW), ALU.add))
                s(V.tensor_reduce(ps_small[:, 8], lg[:, 0], AX.X, ALU.max))
                s(V.tensor_tensor(lg[:, 2], lg[:, 0], bc(ps_small[:, 8], E), ALU.subtract))
                dve.sem_inc(s_lm, 1)
                s(V.tensor_tensor(lg[:, 1], lg[:, 0], bc(ps_small[:, 8], E), ALU.is_ge))
                s(V.tensor_tensor(lg[:, 0], lg[:, 1], rows(cst[0:ROWS, C_RAMP:C_RAMP + E], GW), ALU.mult))
                s(V.tensor_reduce(ps_small[:, 9], lg[:, 0], AX.X, ALU.max))
                s(V.tensor_tensor(oh_all[:, blk], lg[:, 0], bc(ps_small[:, 9], E), ALU.is_equal))

            def post_weight(j, s):
                blk = bass.ds(j * GW, GW)
                dve.wait_ge(s_pe, add(j, 1))
                s(V.tensor_reduce(ps_small[:, 10], lg[:, 3], AX.X, ALU.add))
                s(V.reciprocal(ps_small[:, 11], ps_small[:, 10]))
                s(V.tensor_tensor(lgo[:], oh_all[:, blk], bc(ps_small[:, 11], E), ALU.mult))
                dve.sem_inc(s_ohp, 1)
                s(V.tensor_scalar(ohs_all[:, blk], lgo[:], wmax[0:ROWS, 6:7], None, ALU.mult))

            def post_turned(j, s):
                dve.wait_ge(s_oht, add(j, 1))
                V.tensor_copy(ohT[:], pM[0:GW * E, 0:ROWS]).then_inc(s_ohtc, 1)

            def post_yb(j, s):
                dve.wait_ge(s_yb, add(j, 1))
                V.tensor_copy(yb_all[:, bass.ds(j * GW, GW)], pA).then_inc(s_route, 1)
                assert s.n == NPOST

            def sums(j, first):
                for p in range(NPAIR):
                    dve.wait_ge(s_exp, add(j * NPAIR, p + 1))
                    if p == 0:
                        if not first:
                            dve.wait_ge(s_pnum, j)
                        i = V.tensor_copy(esum[:], ex[:, 0])
                    else:
                        dve.wait_ge(s_es, add(j * NPAIR, p))
                        if p < LAST:
                            i = V.tensor_tensor(esum[:], esum[:], ex[:, p % NE], ALU.add)
                        else:
                            i = V.tensor_tensor(esum[0:KT_REST, 0], esum[0:KT_REST, 0],
                                                ex[0:KT_REST, p % NE, 0], ALU.add)
                    i.then_inc(s_es, 1)
                    if not first:
                        if p == 0:
                            s = post_steps(j - 1, 0)
                            post_norm(j - 1, s)
                        if p == 2:
                            post_center(j - 1, s)
                        if p == 4:
                            post_h2(j - 1, s)
                        if p == 6:
                            post_split(j - 1, s, 0)
                        if p == 8:
                            post_route(j - 1, s)
                        if p == 10:
                            post_weight(j - 1, s)
                        if p == 11:
                            post_turned(j - 1, s)
                if not first:
                    post_yb(j - 1, s)

            NFIN = 12

            def combine(j, p):
                dve.wait_ge(s_l2, add(j * E, 2 * p + 4))
                w = ohs_all[:, bass.ds(j * GW, GW), 2 * p:2 * p + 2]
                V.tensor_tensor(yt[:, p], pY[p % 2], bc(w), ALU.mult).then_inc(s_part, 1)

            def last_norm(s, src, k):
                s(V.tensor_reduce(fin_small[:, 6], src, AX.X, ALU.add))
                s(V.scalar_tensor_tensor(fin_t[:, k], bc(fin_small[:, 6]), -1.0 / D, src, ALU.mult, ALU.add))
                s(V.tensor_tensor(fin_t[:, 3], fin_t[:, k], fin_t[:, k], ALU.mult))
                s(V.tensor_reduce(fin_small[:, 7], fin_t[:, 3], AX.X, ALU.add))
                V.tensor_scalar(fin_small[:, 1 + 3 * k], fin_small[:, 7], 1.0 / D, EPS,
                                ALU.mult, ALU.add).then_inc(s_froot_in, 1)

            def finish(j):
                blk = bass.ds(j * GW, GW)
                s = Steps(dvf, j * NFIN)
                h2 = h2_all[:, blk]
                dve.wait_ge(s_ysum, add(j, 1))
                y = ya[:, 5]
                s(V.tensor_tensor(fin_t[:, 2].bitcast(I32), y.bitcast(I32), mask[:], ALU.bitwise_and))
                s(V.tensor_tensor(fin_t[:, 2], fin_t[:, 2], rest[:, 2], ALU.add))
                last_norm(s, fin_t[:, 2], 0)
                last_norm(s, h2, 1)
                dve.wait_ge(s_froot, add(j * 2, 1))
                s(V.tensor_tensor(ok_all[:, blk], fin_t[:, 0], bc(fin_small[:, 2]), ALU.mult))
                dve.wait_ge(s_froot, add(j * 2, 2))
                s(V.tensor_tensor(od_all[:, blk], fin_t[:, 1], bc(fin_small[:, 5]), ALU.mult))
                assert s.n == NFIN

            step(V.memset(ones_run[:], 1.0))

            sums(0, True)
            with dve.Fori(1, NB - 1) as j:
                sums(j, False)
                for p in range(4):
                    combine(j - 1, p)
                finish(j - 1)
            sums(NB - 1, False)
            last, s = NB - 1, post_steps(NB - 1, 0)
            post_norm(last, s)
            combine(NB - 2, 0)
            post_center(last, s)
            post_h2(last, s)
            combine(NB - 2, 1)
            post_split(last, s, 1)
            post_route(last, s)
            post_weight(last, s)
            combine(NB - 2, 2)
            post_turned(last, s)
            combine(NB - 2, 3)
            post_yb(last, s)

            step(V.tensor_copy(ohe[:], oh_all[:].rearrange("p w e -> p e w")))
            step(V.tensor_reduce(rk_small[:, 0], ohe[:], AX.X, ALU.add))
            dve.sem_inc(s_cnt_in, 1)
            step(V.tensor_tensor_scan(pre[:].rearrange("p e w -> p (e w)"), ones_run[:],
                                      ohe[:].rearrange("p e w -> p (e w)"), 0.0, ALU.mult, ALU.add))
            finish(NB - 2)
            dve.wait_ge(s_cnt, 1)
            step(V.tensor_copy(rk_small[:, 1:3].rearrange("p a e -> p (a e)"), pM[0:ROWS, 0:2 * E]))
            step(V.tensor_tensor(rk_small[:, 1, 1:E], rk_small[:, 1, 1:E], pre[:, 0:E - 1, W - 1], ALU.subtract))
            step(V.tensor_tensor(rk[:, 0], pre[:].rearrange("p e w -> p w e"), rows(rk_small[:, 1], W), ALU.add))
            step(V.tensor_tensor(rk[:, 1], rk[:, 0], oh_all[:], ALU.mult))
            step(V.tensor_reduce(rkw[:, 0], rk[:, 1], AX.X, ALU.add))
            step(V.tensor_tensor(rk[:, 2], oh_all[:], rows(rk_small[:, 2], W), ALU.mult))
            step(V.tensor_reduce(rkw[:, 1], rk[:, 2], AX.X, ALU.add))
            for c in range(COPIES):
                step(V.scalar_tensor_tensor(rkw[:, 2], rkw[:, 1], float(c), rkw[:, 0], ALU.mult, ALU.add))
                step(V.tensor_scalar(kept[:, c], rkw[:, 2], float(CAP), None, ALU.is_le))

            def choose(c, q):
                step(V.tensor_copy(o_all[:, c, q], od_all[:, q]))
                V.copy_predicated(o_all[:, c, q], bc(kept[:, c, q].bitcast(U32)), ok_all[:, q]).then_inc(s_out, 1)

            ahead = slice(0, LASTW)
            combine(last, 0)
            for c in range(COPIES):
                choose(c, ahead)
                combine(last, c + 1)
            finish(last)
            for c in range(COPIES):
                choose(c, slice(LASTW, W))


_INS = ['x', 'L0_tok_ln1_g', 'L0_tok_ln1_b', 'L0_tok_W1', 'L0_tok_b1', 'L0_tok_ln2_g', 'L0_tok_ln2_b',
        'L0_tok_Wp1', 'L0_tok_bp1', 'L0_tok_lnp_g', 'L0_tok_lnp_b', 'L0_tok_Wp2', 'L0_tok_bp2',
        'L0_ffn_gate_w', 'L0_ffn_gate_b', 'L0_ffn_w1', 'L0_ffn_b1', 'L0_ffn_w2', 'L0_ffn_b2']


def kernel(**inputs):
    import concourse.bacc as bacc
    from concourse.bass_utils import run_bass_kernel_spmd as run

    nc = bacc.Bacc("TRN2", target_bir_lowering=False, num_devices=1)
    arrays = {"in_shape_constants": shape_constants()}
    arrays.update({f"in_{n}": np.ascontiguousarray(inputs[n]) for n in _INS})
    args = [nc.dram_tensor(n, a.shape, mybir.dt.from_np(a.dtype), kind="ExternalInput").ap()
            for n, a in arrays.items()]
    out = nc.dram_tensor("out_h", (B, COPIES * HP * W, D), F32, kind="ExternalOutput").ap()
    vit_layer(nc, *args, out)
    r = run(nc, [arrays], core_ids=[0])
    return r.results[0]["out_h"]
```

```python
from contextlib import ExitStack

import numpy as np

import concourse.bass as bass
from concourse import mybir

F32 = mybir.dt.float32
F16 = mybir.dt.float16
U32 = mybir.dt.uint32
I32 = mybir.dt.int32
ACT = mybir.ActivationFunctionType
ALU = mybir.AluOpType
AX = mybir.AxisListType

B, CH, IMG, PATCH = 4, 3, 224, 8
HP = IMG // PATCH
ROWS = B * HP
W = HP
D = 64
D2 = 2 * D
PD = CH * PATCH * PATCH
HALF = PD // 2
GW = 4
NB = W // GW
BLK = GW * ROWS
T = ROWS * W
COPIES = 3
E = 8
F = 256
FC = F // 128
CAP = -(-5 * COPIES * T // (4 * E))
KT_FULL = T // 128
KT_REST = T - KT_FULL * 128
KT = KT_FULL + 1
NPAIR = KT_FULL // 2 + 1
LAST = NPAIR - 1
LASTW = (NB - 1) * GW
PAIRS = [slice(w, min(w + 2 * GW, W)) for w in range(0, W, 2 * GW)]
EPS = 1e-5
NORM_EPS = 1e-12
BIG = 3.4028234663852886e38
INF_AS = 10000.0
SPLIT = 256.0
WTOP = 8192.0


def layout():
    at, n = {}, 0
    for name, width in (("ident", 128), ("stack", D), ("base", ROWS), ("image", ROWS), ("ramp", E), ("centre", D2),
                        ("pair", 2), ("w1t", 2 * 2 * D), ("g1", 2), ("bl1", 2), ("b1", 1), ("wp1", D), ("g2", 1),
                        ("gp", 1), ("bp", 1), ("wp2", D2), ("bl2", ROWS), ("bp1", D), ("bp2", D), ("gate_b", E),
                        ("gate_w", E), ("eb1", E * FC), ("b2", GW * D)):
        at[name] = slice(n, n + width)
        n += width
    return at, n


AT, PACKED = layout()


def pack(v):
    c = np.zeros((128, PACKED), np.float32)

    def put(name, a):
        c[:a.shape[0], AT[name]] = a.reshape(a.shape[0], -1)

    put("ident", np.eye(128))
    put("stack", np.tile(np.eye(D), (2, 1)))
    b, hp = np.divmod(np.arange(ROWS), HP)
    put("base", COPIES * (b[:, None] < b[None, :]) + (b[:, None] == b[None, :]) * (hp[:, None] < hp[None, :]))
    put("image", b[:, None] == b[None, :])
    put("ramp", np.tile(E - np.arange(E), (128, 1)))
    halves = np.kron(np.eye(2), np.ones((D, D)))
    put("centre", np.eye(D2) - halves / D)
    put("pair", halves[:, [0, D]])

    def twice(a):
        return np.concatenate([a, a])

    def image_order(a):
        return a.reshape(PATCH * PATCH, CH, -1).transpose(1, 0, 2).reshape(2, HALF, -1).transpose(1, 0, 2)

    w = image_order(v["L0_tok_W1"])
    put("w1t", np.stack([w, w], 2))
    put("g1", image_order(v["L0_tok_ln1_g"]))
    put("bl1", image_order(v["L0_tok_ln1_b"]))
    for name, key in (("b1", "tok_b1"), ("g2", "tok_ln2_g"), ("gp", "tok_lnp_g"), ("bp", "tok_lnp_b"), ("wp1", "tok_Wp1")):
        put(name, twice(v["L0_" + key].reshape(D, -1)))
    wp2 = np.zeros((2, D, 2, D), np.float32)
    wp2[0, :, 0] = wp2[1, :, 1] = v["L0_tok_Wp2"]
    put("wp2", wp2.reshape(D2, D2))
    put("bl2", np.tile(v["L0_tok_ln2_b"][:, None], (1, ROWS)))
    for name, key in (("bp1", "tok_bp1"), ("bp2", "tok_bp2"), ("gate_b", "ffn_gate_b")):
        put(name, np.tile(v["L0_" + key], (128, 1)))
    put("gate_w", v["L0_ffn_gate_w"])
    put("eb1", v["L0_ffn_b1"].reshape(E * FC, 128).T)
    b2 = np.zeros((GW, E, GW, D), np.float32)
    for w in range(GW):
        b2[w, :, w] = v["L0_ffn_b2"]
    put("b2", b2.reshape(GW * E, GW * D))
    return c


def add(n, k):
    return n + k if k else n


def vit_layer(nc, packed, x, w1, w2, out):
    with ExitStack() as ctx:
        def sb(name, shape, dt=F32):
            return ctx.enter_context(nc.sbuf_tensor(name, shape, dt))

        def sem(name):
            return ctx.enter_context(nc.semaphore(name))

        pk = sb("pk", [128, PACKED])

        def packed_at(name, n=128):
            return pk[0:n, AT[name]]

        ident = packed_at("ident")
        w1t = packed_at("w1t", HALF).rearrange("p (c k d) -> p c k d", c=2, k=2)
        b2d = packed_at("b2", GW * E)
        img = sb("img", [ROWS, CH * PATCH, W, PATCH])
        xn = sb("xn", [ROWS, W, PD])
        xt = sb("xt", [HALF, 2, 2, BLK])
        stats = sb("stats", [ROWS, W, 6])
        ones_col = sb("ones_col", [128, 1])
        half_neg = sb("half_neg", [ROWS, W])
        w1g = sb("w1g", [HALF, 2, D])
        wp1g = sb("wp1g", [D2, D])
        wp1d = sb("wp1d", [D2, 2, D])
        wp2h = sb("wp2h", [D2, D2])
        b1c = sb("b1c", [D2, 2])
        bias2 = sb("bias2", [ROWS, D])
        cen = sb("cen", [128, 8])
        ew1 = sb("ew1", [128, E, F])
        ew1s = sb("ew1s", [128, E, F])
        ew1h = sb("ew1h", [128, E, F], F16)
        ew1l = sb("ew1l", [128, E, F], F16)
        ew2 = sb("ew2", [128, E * FC, D])
        eb1s = sb("eb1s", [128, E * FC])
        wmax = sb("wmax", [128, 8])
        room = sb("room", [ROWS, 3 * W * D])

        def part(at, *shape):
            n, axes = 1, " ".join(f"a{i}" for i in range(len(shape)))
            for k in shape:
                n *= k
            return room[:, at:at + n].rearrange(f"p ({axes}) -> p {axes}", **{f"a{i}": k for i, k in enumerate(shape)})

        ta, tb, tc = (part(k * W * D, W, D) for k in range(3))
        h_all = sb("h_all", [ROWS, W, D])
        f_all = sb("f_all", [ROWS, W, D])
        fdup = img[:].rearrange("p q w r -> p (q w r)")[:, 0:W * 2 * D].rearrange("p (w a d) -> p w a d", a=2, d=D)
        small = sb("small", [ROWS, 12, W])
        fT = xn[0:D].rearrange("p w f -> p (w f)")[:, 0:T]
        QH = sb("QH", [128, T], F16)
        QL = sb("QL", [128, T], F16)
        KHL = sb("KHL", [128, KT * 128], F16)

        def before(ap, at, n):
            k = at * 2 * ROWS
            return ap[:].bitcast(F32)[:, k:k + n * 2 * ROWS].rearrange("p (n t) -> p n t", n=n)

        ucols = before(QH, 0, NB)
        zc = before(QL, 0, 2)
        th = before(QL, 2, 2)
        sc = before(QL, 4, 2)
        usq = before(KHL, 0, 2)
        f2 = sb("f2", [128, KT_FULL + 1, D])
        NE = 3
        ex = sb("ex", [128, NE, 2, BLK])
        esum = sb("esum", [128, 2, BLK])
        att = sb("att", [128, BLK])
        h2row = sb("h2row", [ROWS, GW, D])
        h2dup = sb("h2dup", [ROWS, GW, 2, D])
        xcol = sb("xcol", [128, BLK])
        xhl = sb("xhl", [128, 2, BLK], F16)
        lg = sb("lg", [ROWS, 4, GW, E])
        lgo = sb("lgo", [ROWS, GW, E])
        ones_run = sb("ones_run", [ROWS, E * W])
        ps_small = sb("ps_small", [ROWS, 12, GW])
        ohT = sb("ohT", [GW * E, ROWS])
        oh_all = sb("oh_all", [ROWS, W, E])
        ohs_all = sb("ohs_all", [ROWS, W, E])
        yb_all = sb("yb_all", [ROWS, W, D])
        h2_all = sb("h2_all", [ROWS, W, D])
        hm = ew1s[:].rearrange("p e f -> p (e f)")[:, 0:4 * BLK].rearrange("p (n t) -> p n t", n=4)
        yt = part(0, 4, GW, 2, D)
        ya = part(8 * GW * D, 6, GW, D)
        pt = part(14 * GW * D, 4, GW, D)
        rest = part(18 * GW * D, 3, GW, D)
        zeros = sb("zeros", [ROWS, GW, D])
        mask = sb("mask", [ROWS, GW, D], I32)
        fin_small = sb("fin_small", [ROWS, 8, GW])
        fin_t = sb("fin_t", [ROWS, 4, GW, D])
        outcomes = img[:].rearrange("p q w r -> p (q w r)").rearrange("p (k w d) -> p k w d", k=3, d=D)
        ok_all, od_all = outcomes[:, 0], outcomes[:, 1]
        ohe = sb("ohe", [ROWS, E, W])
        pre = sb("pre", [ROWS, E, W])
        rk = sb("rk", [ROWS, 3, W, E])
        rk_small = sb("rk_small", [ROWS, 4, E])
        kept = sb("kept", [ROWS, COPIES, W])
        rkw = sb("rkw", [ROWS, 3, W])
        o_all = xn[:].rearrange("p w f -> p (w f)").rearrange("p (c w d) -> p c w d", c=COPIES, d=D)

        pS = ctx.enter_context(nc.psum_tensor("pS", [128, 4, 512], F32))
        pR = ctx.enter_context(nc.psum_tensor("pR", [128, 4, 512], F32))
        pAV = pR[:, 0, 0:BLK]
        pY = [pR[0:ROWS, 1 + i, :].rearrange("p (w e d) -> p w e d", w=GW, e=2) for i in range(2)]
        pM = pR[:, 3, :]
        pA = pM[0:ROWS, 0:GW * D].rearrange("p (w d) -> p w d", d=D)
        pDen = pM[0:ROWS, GW * D:GW * D + GW]
        pLog = pM[0:ROWS, 0:GW * E].rearrange("p (w e) -> p w e", e=E)

        ld_img, ld_pack, ld_w1, ld_w2 = (sem(n) for n in ("ld_img", "ld_pack", "ld_w1", "ld_w2"))
        zeroed = sem("zeroed")
        dv = sem("dv")
        dvp = sem("dvp")
        dvf = sem("dvf")
        s_proot_in, s_proot = sem("s_proot_in"), sem("s_proot")
        s_froot_in, s_froot = sem("s_froot_in"), sem("s_froot")
        s_wts = sem("s_wts")
        s_bias = sem("s_bias")
        s_b1 = sem("s_b1")
        s_b1c = sem("s_b1c")
        s_biasc = sem("s_biasc")
        s_wmax_in, s_wmax = sem("s_wmax_in"), sem("s_wmax")
        s_wscale = sem("s_wscale")
        s_wcut = sem("s_wcut")
        s_xn = sem("s_xn")
        s_tr = sem("s_tr")
        s_trc = sem("s_trc")
        s_mm = sem("s_mm")
        s_u = sem("s_u")
        s_ssq = sem("s_ssq")
        s_mm1 = sem("s_mm1")
        s_p = sem("s_p")
        s_sq = sem("s_sq")
        s_z = sem("s_z")
        s_zt = sem("s_zt")
        s_zc = sem("s_zc")
        s_sc = sem("s_sc")
        s_mm2 = sem("s_mm2")
        s_h = sem("s_h")
        s_hsq = sem("s_hsq")
        s_f = sem("s_f")
        s_fd = sem("s_fd")
        s_ft = sem("s_ft")
        s_ftc = sem("s_ftc")
        s_ql = sem("s_ql")
        s_khl = sem("s_khl")
        s_f2 = sem("s_f2")
        s_f2c = sem("s_f2c")
        s_S = sem("s_S")
        s_exp = sem("s_exp")
        s_es = sem("s_es")
        s_av = sem("s_av")
        s_att = sem("s_att")
        s_pnum = sem("s_pnum")
        s_h2 = sem("s_h2")
        s_h2d = sem("s_h2d")
        s_h2t = sem("s_h2t")
        s_xh = sem("s_xh")
        s_x16 = sem("s_x16")
        s_log = sem("s_log")
        s_lm = sem("s_lm")
        s_pe = sem("s_pe")
        s_ohp = sem("s_ohp")
        s_oht = sem("s_oht")
        s_ohtc = sem("s_ohtc")
        s_yb = sem("s_yb")
        s_route = sem("s_route")
        s_l1 = sem("s_l1")
        s_relu = sem("s_relu")
        s_l2 = sem("s_l2")
        s_part = sem("s_part")
        s_ysum = sem("s_ysum")
        pls = sem("pls")
        s_cnt_in, s_cnt = sem("s_cnt_in"), sem("s_cnt")
        s_out = sem("s_out")
        st_out = sem("st_out")

        ctx.enter_context(nc.allow_non_contiguous_dma(reason="a few hundred gains and biases, one to a partition"))
        block = ctx.enter_context(nc.Block())

        img_src = x.rearrange("b c (h q) w -> b h c (q w)", q=PATCH)

        def load_image(eng, b):
            for c in range(CH):
                dst = img[b * HP:(b + 1) * HP, c * PATCH:(c + 1) * PATCH].rearrange("p q w r -> p (q w r)")
                eng.dma_start(dst, img_src[b, :, c]).then_inc(ld_img, 16)

        @block.sync
        def _(sp):
            for b in (0, 1, 2, 3):
                load_image(sp, b)
            for half in range(2):
                sp.dma_start(ew1[half * D:(half + 1) * D], w1.rearrange("e d f -> d e f")).then_inc(ld_w1, 16)
            sp.dma_start(ew2[:], w2.rearrange("e (c p) d -> p (e c) d", p=128)).then_inc(ld_w2, 16)
            for n, (w0, w1_) in enumerate(((0, LASTW), (LASTW, W))):
                for c in range(COPIES):
                    sp.wait_ge(s_out, n * COPIES + c + 1)
                    for b in range(B):
                        dst = out[b].rearrange("(c h w) d -> c h (w d)", c=COPIES, h=HP)[c]
                        src = o_all[b * HP:(b + 1) * HP, c, w0:w1_].rearrange("p w d -> p (w d)")
                        sp.dma_start(dst[:, w0 * D:w1_ * D], src).then_inc(st_out, 16)
            sp.wait_ge(st_out, 2 * 16 * COPIES * B)

        @block.gpsimd
        def _(pool):
            nc.gpsimd.memset(half_neg[:], -0.5).then_inc(zeroed, 1)
            nc.gpsimd.memset(ones_col[:], 1.0).then_inc(zeroed, 1)
            nc.gpsimd.memset(wp1d[:], 0.0).then_inc(zeroed, 1)
            nc.gpsimd.memset(KHL[:, T:KT * 128], 0.0).then_inc(zeroed, 1)
            pool.wait_ge(zeroed, 4)
            nc.gpsimd.memset(f2[KT_REST:128, KT_FULL], 0.0).then_inc(zeroed, 1)
            pool.wait_ge(zeroed, 5)
            nc.gpsimd.memset(zeros[:], 0.0).then_inc(zeroed, 1)
            pool.wait_ge(s_wmax_in, 1)
            nc.gpsimd.partition_all_reduce(wmax[:, 1:2], wmax[:, 0:1], 128,
                                           bass.bass_isa.ReduceOp.max).then_inc(s_wmax, 1)

            pool.wait_ge(s_wscale, 1)
            nc.gpsimd.tensor_scalar(ew1s[:], ew1[:], wmax[:, 4:5], None, ALU.mult).then_inc(s_wcut, 1)
            pool.wait_ge(s_wcut, 1)
            nc.gpsimd.tensor_copy(ew1h[:], ew1s[:]).then_inc(s_wcut, 1)
            pool.wait_ge(s_wcut, 2)
            nc.gpsimd.tensor_tensor(ew1l[:], ew1s[:], ew1h[:], ALU.subtract).then_inc(s_wcut, 1)

            def roots(n, src, dst, sin, sout):
                pool.wait_ge(sin, add(n, 1))
                nc.gpsimd.tensor_tensor(dst, src, half_neg[:, 0:GW], ALU.pow).then_inc(sout, 1)

            def post(j):
                roots(2 * j, ps_small[:, 1], ps_small[:, 2], s_proot_in, s_proot)
                roots(2 * j + 1, ps_small[:, 4], ps_small[:, 5], s_proot_in, s_proot)

            def expert_sums(j):
                base = j * 13
                for p in range(4):
                    pool.wait_ge(s_part, add(j * 4, p + 3))
                    nc.gpsimd.tensor_tensor(ya[:, p], yt[:, p, :, 0], yt[:, p, :, 1], ALU.add).then_inc(pls, 1)
                    if p:
                        pool.wait_ge(pls, add(base, 2 * p))
                        first = ya[:, 0] if p == 1 else ya[:, 4]
                        nc.gpsimd.tensor_tensor(ya[:, 4], first, ya[:, p], ALU.add).then_inc(pls, 1)
                pool.wait_ge(s_route, add(j, 1))
                pool.wait_ge(pls, add(base, 7))
                nc.gpsimd.tensor_tensor(ya[:, 5], ya[:, 4], yb_all[:, bass.ds(j * GW, GW)], ALU.add).then_inc(pls, 1)

            def finite(j):
                base = j * 13
                y = ya[:, 5]
                pool.wait_ge(pls, add(base, 8))
                nc.gpsimd.tensor_tensor(ya[:, 0], y, zeros[:], ALU.mult).then_inc(pls, 1)
                nc.gpsimd.tensor_scalar(rest[:, 0], y, BIG, INF_AS, ALU.is_gt, ALU.mult).then_inc(pls, 1)
                nc.gpsimd.tensor_scalar(rest[:, 1], y, -BIG, -INF_AS, ALU.is_lt, ALU.mult).then_inc(pls, 1)
                pool.wait_ge(pls, add(base, 11))
                nc.gpsimd.tensor_tensor(rest[:, 0], rest[:, 0], rest[:, 1], ALU.add).then_inc(pls, 1)
                nc.gpsimd.tensor_scalar(mask[:], ya[:, 0], 0.0, -1.0, ALU.is_equal, ALU.mult).then_inc(pls, 1)
                pool.wait_ge(pls, add(base, 13))
                nc.gpsimd.tensor_tensor(rest[:, 2], rest[:, 0], h2_all[:, bass.ds(j * GW, GW)], ALU.add).then_inc(s_ysum, 1)

            def last_roots(j):
                pool.wait_ge(s_froot_in, add(j, 1))
                nc.gpsimd.tensor_tensor(fin_small[:, 2:4], fin_small[:, 0:2],
                                        half_neg[:, 0:2 * GW].rearrange("p (k w) -> p k w", k=2),
                                        ALU.pow).then_inc(s_froot, 1)

            def stage(j):
                post(j - 1)
                finite(j - 2)
                last_roots(j - 2)
                expert_sums(j - 1)

            post(0)
            expert_sums(0)
            with pool.Fori(2, NB - 1) as j:
                stage(j)
            post(NB - 2)
            finite(NB - 3)
            last_roots(NB - 3)
            post(NB - 1)
            expert_sums(NB - 2)
            finite(NB - 2)
            last_roots(NB - 2)
            expert_sums(NB - 1)
            finite(NB - 1)
            last_roots(NB - 1)

        @block.scalar
        def _(act):
            act.dma_start(pk[:], packed).then_inc(ld_pack, 16)
            act.wait_ge(ld_pack, 16)
            for g in range(NB + 1):
                if g < NB:
                    act.wait_ge(s_tr, g + 1)
                    if g >= 2:
                        act.wait_ge(s_mm, g - 1)
                    nc.scalar.copy(xt[:, g % 2], pS[0:HALF, 2 * (g % 2):2 * (g % 2) + 2, 0:BLK]).then_inc(s_trc, 1)
                if g == 0:
                    act.wait_ge(s_biasc, 1)
                if g:
                    k = g - 1
                    act.wait_ge(s_mm, k + 1)
                    nc.scalar.activation(ucols[:, k], pR[:, k % 3, 0:2 * ROWS], ACT.Identity,
                                         bias=b1c[:, 1:2]).then_inc(s_u, 1)
                    if k >= 2:
                        act.wait_ge(s_ssq, k - 1)
                    nc.scalar.activation(usq[:, k % 2], pR[:, k % 3, 0:2 * ROWS], ACT.Square,
                                         bias=b1c[:, 1:2]).then_inc(s_u, 1)
            for k, q in enumerate(PAIRS):
                act.wait_ge(s_p, k + 1)
                nc.scalar.square(tb[:, q], ta[:, q]).then_inc(s_sq, 1)
            for g in range(NB + 3):
                if g < NB:
                    act.wait_ge(s_zt, g + 1)
                    if g >= 2:
                        act.wait_ge(s_sc, g - 1)
                    nc.scalar.activation(zc[:, g % 2], pS[:, g % 4, 0:2 * ROWS], ACT.Identity,
                                         bias=packed_at("bp"), scale=packed_at("gp")).then_inc(s_zc, 1)
                    act.wait_ge(s_zc, 2 * g + 1)
                    nc.scalar.activation(th[:, g % 2], zc[:, g % 2], ACT.Tanh, scale=0.5).then_inc(s_zc, 1)
                if g >= 3:
                    k = g - 3
                    act.wait_ge(s_h, k + 1)
                    q = slice(k * GW, (k + 1) * GW)
                    nc.scalar.square(tb[:, q], h_all[:, q]).then_inc(s_hsq, 1)
            def double(src):
                return src.unsqueeze(2).broadcast_to([ROWS, GW, 2, D])

            def double_f(g):
                act.wait_ge(s_f, g + 1)
                q = slice(g * GW, (g + 1) * GW)
                nc.scalar.copy(fdup[:, q], double(f_all[:, q])).then_inc(s_fd, 1)

            double_f(0)
            for g in range(NB):
                if g + 1 < NB:
                    double_f(g + 1)
                act.wait_ge(s_ft, g + 1)
                nc.scalar.copy(QH[:, g * BLK:(g + 1) * BLK], pS[:, g % 4, 0:BLK]).then_inc(s_ftc, 1)
                nc.scalar.copy(fT[:, g * BLK:(g + 1) * BLK], pS[0:D, g % 4, 0:BLK]).then_inc(s_ftc, 1)
            for g in range(4):
                act.wait_ge(s_f2, g + 1)
                n = 8 if g < 3 else 1
                m = 128 if g < 3 else KT_REST
                nc.scalar.copy(f2[0:m, 8 * g:8 * g + n], pR[0:m, g, 0:n * D].rearrange("p (n d) -> p n d", d=D)).then_inc(s_f2c, 1)

            def exponentials(j, first, lone=False):
                for p in range(NPAIR):
                    act.wait_ge(s_S, add(j * NPAIR, p + 1))
                    if not (first and p < NE):
                        act.wait_ge(s_av, add(j * NPAIR, max(p + 1 - NE, 0)))
                        act.wait_ge(s_es, add(j * NPAIR, max(p + 1 - NE, 0)))
                    if p < LAST:
                        o, i = ex[:, p % NE], pS[:, 2 * (p % 2):2 * (p % 2) + 2, 0:BLK]
                    else:
                        o, i = ex[:, p % NE, 0], pS[:, 2 * (p % 2), 0:BLK]
                    nc.scalar.activation(o, i, ACT.Exp, scale=1.0 / (SPLIT * SPLIT)).then_inc(s_exp, 1)
                    if p == 6 and not first:
                        keep_h2(j - 1)
                    if p == 9 and not first:
                        copy_columns(j - 1, 0)
                act.wait_ge(s_av, add(j * NPAIR, NPAIR))
                if not first:
                    act.wait_ge(s_pnum, j)
                nc.scalar.copy(att[:], pAV).then_inc(s_att, 1)

            def keep_h2(j):
                act.wait_ge(s_h2, add(j, 1))
                nc.scalar.copy(h2dup[:], double(h2row[:])).then_inc(s_h2d, 1)
                nc.scalar.copy(h2_all[:, bass.ds(j * GW, GW)], h2row[:]).then_inc(s_h2d, 1)

            def copy_columns(j, slot):
                act.wait_ge(s_h2t, add(j, 1))
                nc.scalar.copy(xcol[:], pM[:, 0:BLK]).then_inc(s_xh, 1)
                nc.scalar.activation(xhl[:, slot], pM[:, 0:BLK], ACT.Copy, scale=SPLIT).then_inc(s_xh, 1)

            def gate_exp(j):
                act.wait_ge(s_lm, add(j, 1))
                nc.scalar.activation(lg[:, 3], lg[:, 2], ACT.Exp).then_inc(s_pe, 1)

            def relus(j, last_post=False):
                for c in range(E * FC):
                    act.wait_ge(s_l1, add(j * E * FC, c + 1))
                    act.wait_ge(s_l2, add(j * E, c // FC + 1))
                    nc.scalar.activation(hm[:, c % 4], pS[:, c % 4, 0:BLK], ACT.Relu, bias=eb1s[:, c:c + 1]).then_inc(s_relu, 1)
                    if c == 1:
                        gate_exp(j)
                    if c == 5:
                        act.wait_ge(s_oht, add(j, 1))
                        nc.scalar.copy(ohT[:], pM[0:GW * E, 0:ROWS]).then_inc(s_ohtc, 1)
                    if c == 7:
                        act.wait_ge(s_yb, add(j, 1))
                        nc.scalar.copy(yb_all[:, bass.ds(j * GW, GW)], pA).then_inc(s_route, 1)
                    if c == 11 and last_post:
                        keep_h2(NB - 1)
                    if c == 14 and last_post:
                        copy_columns(NB - 1, 1)

            act.wait_ge(s_wscale, 1)
            exponentials(0, True)
            exponentials(1, False)
            relus(0)
            with act.Fori(2, NB - 1) as j:
                exponentials(j, False)
                relus(j - 1)
            exponentials(NB - 1, False)
            relus(NB - 2, last_post=True)
            relus(NB - 1)

        @block.tensor
        def _(pe):
            MM = pe.matmul
            pe.sem_inc(s_l2, 2)
            pe.wait_ge(ld_pack, 16)
            for c in range(2):
                MM(pR[:, 3, 64:65], w1t[:, c].rearrange("p k d -> p (k d)"), packed_at("bl1", HALF)[:, c:c + 1],
                   start=(c == 0), stop=(c == 1))
            MM(pR[0:ROWS, 3, 128:128 + D], packed_at("bl2", D), packed_at("wp1", D), start=True, stop=True).then_inc(s_bias, 1)
            pe.wait_ge(s_b1, 1)
            MM(pR[:, 3, 65:66], packed_at("centre"), b1c[:, 0:1], start=True, stop=True).then_inc(s_b1c, 1)

            def tokenize(g):
                pe.wait_ge(s_xn, g + 1)
                if g >= 2:
                    pe.wait_ge(s_trc, g - 1)
                for w in range(GW):
                    for c in range(2):
                        i = pe.transpose(pS[0:HALF, 2 * (g % 2) + c, w * ROWS:(w + 1) * ROWS],
                                         xn[:, g * GW + w, c * HALF:(c + 1) * HALF], ident[0:ROWS, 0:ROWS])
                i.then_inc(s_tr, 1)

            def project(g):
                pe.wait_ge(s_trc, g + 1)
                if g == 0:
                    pe.wait_ge(s_wts, 1)
                if g >= 3:
                    pe.wait_ge(s_u, 2 * (g - 2))
                for c in range(2):
                    x2 = xt[:, g % 2, c].rearrange("p (q h r) -> p h q r", q=2, h=2)
                    for h in range(2):
                        i = MM(pR[h * D:(h + 1) * D, g % 3, 0:2 * ROWS], w1g[:, c], x2[:, h],
                               start=(c == 0), stop=(c == 1))
                i.then_inc(s_mm, 1)

            def square_sums(g):
                pe.wait_ge(s_u, 2 * (g + 1))
                if g == 0:
                    pe.wait_ge(s_biasc, 1)
                for q in range(2):
                    w = g * GW + 2 * q
                    i = MM(pR[0:ROWS, 3, w:w + 2], usq[:, g % 2, q * ROWS:(q + 1) * ROWS], packed_at("pair"),
                           start=True, stop=True)
                i.then_inc(s_ssq, 1)

            for g in range(NB + 2):
                if g < NB:
                    tokenize(g)
                if 1 <= g <= NB:
                    project(g - 1)
                if g >= 2:
                    square_sums(g - 2)
            pe.wait_ge(s_trc, NB)
            for g in range(NB):
                for q in range(2):
                    o = (g % 2) * GW * D + q * D2
                    i = MM(pS[0:ROWS, g // 2, o:o + D2], ucols[:, g, q * ROWS:(q + 1) * ROWS],
                           wp1d[:].rearrange("p h d -> p (h d)"), start=True, stop=True)
            i.then_inc(s_mm1, 1)
            for g in range(NB + 1):
                if g < NB:
                    pe.wait_ge(s_z, g // 2 + 1)
                    if g >= 4:
                        pe.wait_ge(s_zc, 2 * (g - 4) + 1)
                    elif g:
                        pe.wait_ge(s_p, g + 1)
                    for q in range(2):
                        w = g * GW + 2 * q
                        i = pe.transpose(pS[:, g % 4, q * ROWS:(q + 1) * ROWS],
                                         tc[:, w:w + 2].rearrange("p w d -> p (w d)"), ident[0:ROWS, 0:ROWS])
                    i.then_inc(s_zt, 1)
                if g:
                    k = g - 1
                    pe.wait_ge(s_sc, k + 1)
                    if k >= 4:
                        pe.wait_ge(s_h, k - 3)
                    for q in range(2):
                        i = MM(pR[0:ROWS, k % 4, q * D2:(q + 1) * D2], sc[:, k % 2, q * ROWS:(q + 1) * ROWS], wp2h[:],
                               start=True, stop=True)
                    i.then_inc(s_mm2, 1)

            for g in range(NB):
                pe.wait_ge(s_fd, g + 1)
                if g >= 4:
                    pe.wait_ge(s_ftc, 2 * (g - 3))
                    pe.wait_ge(s_ql, g - 3)
                for w in range(GW):
                    i = pe.transpose(pS[:, g % 4, w * ROWS:(w + 1) * ROWS], fdup[:, g * GW + w].rearrange("p a d -> p (a d)"),
                                     ident[0:ROWS, 0:ROWS])
                i.then_inc(s_ft, 1)
            pe.wait_ge(s_ftc, 2 * NB)
            pe.wait_ge(s_h, NB)
            for k in range(KT_FULL + 1):
                m = 128 if k < KT_FULL else KT_REST
                i = pe.transpose(pR[0:m, k // 8, (k % 8) * D:(k % 8 + 1) * D], fT[:, k * 128:k * 128 + m],
                                 ident[0:D, 0:D])
                if k % 8 == 7 or k == KT_FULL:
                    i.then_inc(s_f2, 1)

            def scores(j, first, p):
                if p < 2:
                    if not first:
                        pe.wait_ge(s_exp, j * NPAIR)
                else:
                    pe.wait_ge(s_exp, add(j * NPAIR, p - 1))
                tiles = 2 if p < LAST else 1
                for t in range(tiles):
                    k0 = (2 * p + t) * 128
                    o = pS[:, 2 * (p % 2) + t, 0:BLK]
                    MM(o, KHL[:, k0:k0 + 128], QH[:, bass.ds(j * BLK, BLK)], start=True, stop=False)
                    i = MM(o, KHL[:, k0:k0 + 128], QL[:, bass.ds(j * BLK, BLK)], start=False, stop=True)
                i.then_inc(s_S, 1)

            def values(j, first, p):
                pe.wait_ge(s_exp, add(j * NPAIR, p + 1))
                if p == 0 and not first:
                    pe.wait_ge(s_att, j)
                if p < LAST:
                    for t in range(2):
                        i = MM(pR[t * D:(t + 1) * D, 0, 0:BLK], f2[:, 2 * p + t], ex[:, p % NE, t],
                               start=(p == 0), stop=(p == LAST - t))
                else:
                    i = MM(pR[0:D, 0, 0:BLK], f2[:, 2 * p], ex[:, p % NE, 0],
                           start=False, stop=True)
                i.then_inc(s_av, 1)

            def post_sums(j):
                pe.wait_ge(s_es, add(j * NPAIR, NPAIR))
                pe.wait_ge(s_att, add(j, 1))
                if not (isinstance(j, int) and j == 0):
                    pe.wait_ge(s_route, j)
                for w in range(GW):
                    q = slice(w * ROWS, (w + 1) * ROWS)
                    for t in range(2):
                        MM(pDen[:, w:w + 1], esum[:, t, q], ones_col[:], start=(t == 0), stop=(t == 1))
                for w in range(GW):
                    q = slice(w * ROWS, (w + 1) * ROWS)
                    i = MM(pA[:, w], att[:, q], packed_at("stack"), start=True, stop=True)
                i.then_inc(s_pnum, 1)

            def post_cols(j):
                pe.wait_ge(s_h2d, add(j * 2, 2))
                for w in range(GW):
                    i = pe.transpose(pM[:, w * ROWS:(w + 1) * ROWS], h2dup[:, w].rearrange("p a d -> p (a d)"),
                                     ident[0:ROWS, 0:ROWS])
                i.then_inc(s_h2t, 1)

            def post_gate(j):
                pe.wait_ge(s_x16, add(j, 1))
                for w in range(GW):
                    i = MM(pLog[:, w], xcol[:, w * ROWS:(w + 1) * ROWS], packed_at("gate_w"), start=True, stop=True)
                i.then_inc(s_log, 1)

            def post_turn(j):
                pe.wait_ge(s_ohp, add(j, 1))
                pe.transpose(pM[0:GW * E, 0:ROWS], lgo[:].rearrange("p w e -> p (w e)"),
                             ident[0:ROWS, 0:ROWS]).then_inc(s_oht, 1)

            def post_b2(j):
                pe.wait_ge(s_ohtc, add(j, 1))
                MM(pA.rearrange("p w d -> p (w d)"), ohT[:], b2d,
                   start=True, stop=True).then_inc(s_yb, 1)

            def attention(j, first):
                for p in range(NPAIR + 1):
                    if p < NPAIR:
                        scores(j, first, p)
                    if p:
                        values(j, first, p - 1)
                    if not first:
                        if p == 0:
                            post_sums(j - 1)
                        if p == 8:
                            post_cols(j - 1)
                        if p == NPAIR:
                            post_gate(j - 1)

            def hidden(j, c, slot):
                if c >= 4:
                    pe.wait_ge(s_relu, add(j * E * FC, c - 3))
                o = pS[:, c % 4, 0:BLK]
                e, k = c // FC, (c % FC) * 128
                MM(o, ew1h[:, e, k:k + 128], xhl[:, slot], start=True, stop=False)
                MM(o, ew1l[:, e, k:k + 128], xhl[:, slot], start=False, stop=True).then_inc(s_l1, 1)

            def outputs(j, e):
                pe.wait_ge(s_relu, add(j * E * FC, FC * e + FC))
                if e % 2 == 0:
                    pe.wait_ge(s_part, add(j * 4, e // 2 + 1))
                for w in range(GW):
                    for c in range(FC):
                        i = MM(pY[(e // 2) % 2][:, w, e % 2], hm[:, (FC * e + c) % 4, w * ROWS:(w + 1) * ROWS],
                               ew2[:, FC * e + c], start=(c == 0), stop=(c == FC - 1))
                i.then_inc(s_l2, 1)

            def queue_bases():
                pe.wait_ge(s_route, NB)
                pe.wait_ge(s_cnt_in, 1)
                MM(pM[0:ROWS, 0:E], packed_at("base", ROWS), rk_small[:, 0], start=True, stop=True)
                MM(pM[0:ROWS, E:2 * E], packed_at("image", ROWS), rk_small[:, 0],
                   start=True, stop=True).then_inc(s_cnt, 1)

            def experts(j, last_post=False, slot=0):
                j_is_last = slot == 1
                pe.wait_ge(s_exp, NPAIR * NB if j_is_last else add(j * NPAIR, 2 * NPAIR))
                if j_is_last:
                    pe.wait_ge(s_relu, j * E * FC)
                pe.wait_ge(s_x16, add(j, 1))
                for e in range(E + 1):
                    if e < E:
                        for c in range(FC):
                            hidden(j, FC * e + c, slot)
                    if e:
                        outputs(j, e - 1)
                    if e == 2:
                        post_turn(j)
                    if e == 3:
                        post_b2(j)
                    if last_post:
                        if e == 4:
                            post_sums(NB - 1)
                        if e == 7:
                            post_cols(NB - 1)
                        if e == 8:
                            post_gate(NB - 1)
                    if j_is_last and e == 4:
                        queue_bases()

            pe.wait_ge(s_khl, 2 * NB)
            pe.wait_ge(zeroed, 5)
            pe.wait_ge(s_f2c, 4)
            attention(0, True)
            pe.wait_ge(ld_w2, 16)
            pe.wait_ge(s_wcut, 3)
            attention(1, False)
            experts(0)
            with pe.Fori(2, NB - 1) as j:
                attention(j, False)
                experts(j - 1)
            attention(NB - 1, False)
            experts(NB - 2, last_post=True)
            experts(NB - 1, slot=1)

        @block.vector
        def _(dve):
            V = nc.vector

            class Steps:

                def __init__(self, s, base=0):
                    self.s, self.base, self.n = s, base, 0

                def __call__(self, ins):
                    self.n += 1
                    ins.then_inc(self.s, 1)
                    dve.wait_ge(self.s, add(self.base, self.n))

            step = Steps(dv)

            def bc(ap, n=D):
                return ap.unsqueeze(ap.ndim).broadcast_to([*ap.shape, n])

            def rows(v, n):
                return v.unsqueeze(1).broadcast_to([ROWS, n, v.shape[-1]])

            dve.sem_inc(s_part, 2)

            def inverse_root(x, y, t):
                step(V.tensor_scalar(t.bitcast(I32), x.bitcast(I32), 1, None, ALU.logical_shift_right))
                step(V.tensor_scalar(y.bitcast(I32), t.bitcast(I32), -1.0, float(0x5F3759DF), ALU.mult, ALU.add))
                for _ in range(3):
                    step(V.scalar_tensor_tensor(t, y, -0.5, y, ALU.mult, ALU.mult))
                    step(V.tensor_tensor(t, t, x, ALU.mult))
                    step(V.scalar_tensor_tensor(y, t, 1.5, y, ALU.add, ALU.mult))

            dve.wait_ge(ld_pack, 16)
            g1, g2 = packed_at("g1", HALF), packed_at("g2")
            for c in range(2):
                step(V.tensor_scalar(w1g[:, c], w1t[:, c, 0], g1[:, c:c + 1], None, ALU.mult))
            step(V.tensor_reduce(cen[0:HALF, 0:2], w1g[:], AX.X, ALU.add))
            step(V.tensor_scalar(cen[0:HALF, 2:4], cen[0:HALF, 0:2], 1.0 / D, None, ALU.mult))
            for c in range(2):
                step(V.tensor_scalar(w1g[:, c], w1g[:, c], cen[0:HALF, 2 + c:3 + c], None, ALU.subtract))
            step(V.tensor_scalar(wp1g[:], packed_at("wp1"), g2, None, ALU.mult))
            step(V.tensor_reduce(cen[:, 4:5], wp1g[:], AX.X, ALU.add))
            step(V.tensor_scalar(cen[:, 5:6], cen[:, 4:5], 1.0 / D, None, ALU.mult))
            dve.wait_ge(zeroed, 3)
            for half in range(2):
                r = slice(half * D, (half + 1) * D)
                step(V.tensor_scalar(wp1d[r, half], wp1g[r], cen[r, 5:6], None, ALU.subtract))
            step(V.tensor_scalar(wp2h[:], packed_at("wp2"), 0.5, None, ALU.mult))
            dve.sem_inc(s_wts, 1)
            dve.wait_ge(s_bias, 1)
            step(V.tensor_tensor(b1c[:, 0:1], pR[:, 3, 64:65], packed_at("b1"), ALU.add))
            step(V.tensor_tensor(bias2[:], pR[0:ROWS, 3, 128:128 + D], packed_at("bp1", ROWS), ALU.add))
            dve.sem_inc(s_b1, 1)
            step(V.tensor_reduce(cen[0:ROWS, 6:7], bias2[:], AX.X, ALU.add))
            step(V.tensor_scalar(cen[0:ROWS, 7:8], cen[0:ROWS, 6:7], 1.0 / D, None, ALU.mult))
            step(V.tensor_scalar(bias2[:], bias2[:], cen[0:ROWS, 7:8], None, ALU.subtract))
            dve.wait_ge(s_b1c, 1)
            step(V.tensor_copy(b1c[:, 1:2], pR[:, 3, 65:66]))
            dve.sem_inc(s_biasc, 1)

            def first_norm(w0, w1_):
                for w in range(w0, w1_):
                    i = V.bn_stats(stats[:, w], img[:, :, w, :])
                step(i)
                me, mo, ve, vo = (stats[:, w0:w1_, k] for k in (1, 4, 2, 5))
                var, r, t, dif, dif2, vsum, mu = (small[:, k, w0:w1_] for k in (0, 1, 11, 8, 9, 10, 7))
                step(V.tensor_tensor(dif, me, mo, ALU.subtract))
                step(V.tensor_tensor(t, me, mo, ALU.add))
                step(V.tensor_tensor(dif2, dif, dif, ALU.mult))
                step(V.tensor_tensor(vsum, ve, vo, ALU.add))
                step(V.tensor_scalar(dif2, dif2, 0.25, EPS, ALU.mult, ALU.add))
                step(V.scalar_tensor_tensor(var, vsum, 1.0 / PD, dif2, ALU.mult, ALU.add))
                step(V.tensor_scalar(mu, t, 0.5, None, ALU.mult))
                inverse_root(var, r, t)
                for w in range(w0, w1_):
                    i = V.tensor_scalar(xn[:, w].rearrange("p (a r) -> p a r", r=PATCH), img[:, :, w, :],
                                        small[:, 7, w:w + 1], small[:, 1, w:w + 1], ALU.subtract, ALU.mult)
                    if w % GW == GW - 1:
                        i.then_inc(s_xn, 1)

            dve.wait_ge(ld_img, CH * B * 16)
            first_norm(0, 3 * GW)
            first_norm(3 * GW, W)

            dve.wait_ge(ld_w1, 32)
            V.tensor_reduce(wmax[:, 0:1], ew1[:].rearrange("p e f -> p (e f)"), AX.X, ALU.max,
                            apply_absolute_value=True).then_inc(s_wmax_in, 1)

            x_, y_, t_ = small[:, 2], small[:, 3], small[:, 11]
            dve.wait_ge(s_ssq, NB)
            step(V.tensor_scalar(x_, pR[0:ROWS, 3, 0:W], 1.0 / D, EPS, ALU.mult, ALU.add))
            inverse_root(x_, y_, t_)
            dve.wait_ge(s_mm1, 1)
            for k, q in enumerate(PAIRS):
                n = q.stop - q.start
                u = pS[0:ROWS, k, 0:n * D].rearrange("p (w d) -> p w d", d=D)
                step(V.tensor_tensor(tc[:, q], u, bc(y_[:, q]), ALU.mult))
                V.tensor_tensor(ta[:, q], tc[:, q], rows(bias2[:], n), ALU.add).then_inc(s_p, 1)
            for k, q in enumerate(PAIRS):
                dve.wait_ge(s_sq, k + 1)
                i = V.tensor_reduce(small[:, 9, q], tb[:, q], AX.X, ALU.add)
            step(i)
            x_, y_ = small[:, 4], small[:, 5]
            step(V.tensor_scalar(x_, small[:, 9], 1.0 / D, EPS, ALU.mult, ALU.add))
            inverse_root(x_, y_, t_)
            for q in PAIRS:
                V.tensor_tensor(tc[:, q], ta[:, q], bc(y_[:, q]), ALU.mult).then_inc(s_z, 1)
            dve.wait_ge(s_wmax, 1)
            step(V.tensor_scalar(wmax[:, 2:3], wmax[:, 1:2], 1e-30, None, ALU.max))
            step(V.tensor_scalar(wmax[:, 3:4].bitcast(I32), wmax[:, 2:3].bitcast(I32), 0x7F800000, None,
                                 ALU.bitwise_and))
            step(V.reciprocal(wmax[:, 5:6], wmax[:, 3:4]))
            step(V.tensor_scalar(wmax[:, 4:5], wmax[:, 5:6], WTOP, None, ALU.mult))
            step(V.tensor_scalar(wmax[:, 6:7], wmax[:, 3:4], 1.0 / (WTOP * SPLIT), None, ALU.mult))
            step(V.tensor_scalar(eb1s[:], packed_at("eb1"), wmax[:, 4:5], SPLIT, ALU.mult, ALU.mult))
            dve.sem_inc(s_wscale, 1)
            for g in range(NB + 1):
                if g < NB:
                    dve.wait_ge(s_zc, 2 * (g + 1))
                    if g >= 2:
                        dve.wait_ge(s_mm2, g - 1)
                    V.scalar_tensor_tensor(sc[:, g % 2], th[:, g % 2], 1.0, zc[:, g % 2],
                                           ALU.add, ALU.mult).then_inc(s_sc, 1)
                if g:
                    k = g - 1
                    dve.wait_ge(s_mm2, k + 1)
                    u = pR[0:ROWS, k % 4, 0:GW * D].rearrange("p (w d) -> p w d", d=D)
                    V.tensor_tensor(h_all[:, k * GW:(k + 1) * GW], u, rows(packed_at("bp2", ROWS), GW),
                                    ALU.add).then_inc(s_h, 1)
            for g in range(NB):
                q = slice(g * GW, (g + 1) * GW)
                dve.wait_ge(s_hsq, g + 1)
                i = V.tensor_reduce(small[:, 9, q], tb[:, q], AX.X, ALU.add)
            step(i)
            x_, y_ = small[:, 6], small[:, 8]
            step(V.tensor_scalar(x_, small[:, 9], 1e-30, None, ALU.max))
            inverse_root(x_, y_, t_)
            step(V.tensor_scalar(small[:, 10], y_, 1.0 / NORM_EPS, SPLIT, ALU.min, ALU.mult))
            dve.wait_ge(s_h, NB)
            for g in range(NB):
                q = slice(g * GW, (g + 1) * GW)
                V.tensor_tensor(f_all[:, q], h_all[:, q], bc(small[:, 10, q]), ALU.mult).then_inc(s_f, 1)
            for g in range(NB):
                q = slice(g * BLK, (g + 1) * BLK)
                dve.wait_ge(s_ftc, 2 * (g + 1))
                V.tensor_tensor(QL[:, q], pS[:, g % 4, 0:BLK], QH[:, q], ALU.subtract).then_inc(s_ql, 1)
                V.tensor_copy(KHL[0:D, q], QH[0:D, q]).then_inc(s_khl, 1)
                dve.wait_ge(s_ql, g + 1)
                V.tensor_copy(KHL[D:D2, q], QL[D:D2, q]).then_inc(s_khl, 1)

            NPOST = 25

            def post_steps(j, at):
                s = Steps(dvp, j * NPOST)
                s.n = at
                return s

            def post_norm(j, s):
                blk = bass.ds(j * GW, GW)
                dve.wait_ge(s_pnum, add(j, 1))
                s(V.reciprocal(ps_small[:, 0], pDen))
                s(V.tensor_scalar(ps_small[:, 0], ps_small[:, 0], 0.2, None, ALU.mult))
                s(V.tensor_tensor(pt[:, 0], pA, bc(ps_small[:, 0]), ALU.mult))
                s(V.scalar_tensor_tensor(pt[:, 1], f_all[:, blk], 0.8, pt[:, 0], ALU.mult, ALU.add))
                s(V.tensor_tensor(pt[:, 2], pt[:, 1], pt[:, 1], ALU.mult))
                V.tensor_reduce(ps_small[:, 1], pt[:, 2], AX.X, ALU.add).then_inc(s_proot_in, 1)

            def post_center(j, s):
                blk = bass.ds(j * GW, GW)
                dve.wait_ge(s_proot, add(j * 2, 1))
                s(V.tensor_scalar(ps_small[:, 3], ps_small[:, 2], 1.0 / (NORM_EPS * SPLIT), None, ALU.min))
                s(V.tensor_tensor(pt[:, 0], pt[:, 1], bc(ps_small[:, 3]), ALU.mult))
                s(V.tensor_tensor(pt[:, 1], pt[:, 0], h_all[:, blk], ALU.add))
                s(V.tensor_reduce(ps_small[:, 6], pt[:, 1], AX.X, ALU.add))
                s(V.scalar_tensor_tensor(pt[:, 2], bc(ps_small[:, 6]), -1.0 / D, pt[:, 1], ALU.mult, ALU.add))
                s(V.tensor_tensor(pt[:, 3], pt[:, 2], pt[:, 2], ALU.mult))
                s(V.tensor_reduce(ps_small[:, 7], pt[:, 3], AX.X, ALU.add))
                V.tensor_scalar(ps_small[:, 4], ps_small[:, 7], 1.0 / D, EPS, ALU.mult, ALU.add).then_inc(s_proot_in, 1)

            def post_h2(j, s):
                dve.wait_ge(s_proot, add(j * 2, 2))
                s(V.tensor_tensor(h2row[:], pt[:, 2], bc(ps_small[:, 5]), ALU.mult))
                dve.sem_inc(s_h2, 1)

            def post_split(j, s, slot):
                dve.wait_ge(s_xh, add(j * 2, 2))
                s(V.scalar_tensor_tensor(xhl[D:D2, slot], xcol[D:D2], SPLIT, xhl[D:D2, slot],
                                         ALU.mult, ALU.subtract))
                dve.sem_inc(s_x16, 1)

            def post_route(j, s):
                blk = bass.ds(j * GW, GW)
                dve.wait_ge(s_log, add(j, 1))
                s(V.tensor_tensor(lg[:, 0], pLog, rows(packed_at("gate_b", ROWS), GW), ALU.add))
                s(V.tensor_reduce(ps_small[:, 8], lg[:, 0], AX.X, ALU.max))
                s(V.tensor_tensor(lg[:, 2], lg[:, 0], bc(ps_small[:, 8], E), ALU.subtract))
                dve.sem_inc(s_lm, 1)
                s(V.tensor_tensor(lg[:, 1], lg[:, 0], bc(ps_small[:, 8], E), ALU.is_ge))
                s(V.tensor_tensor(lg[:, 0], lg[:, 1], rows(packed_at("ramp", ROWS), GW), ALU.mult))
                s(V.tensor_reduce(ps_small[:, 9], lg[:, 0], AX.X, ALU.max))
                s(V.tensor_tensor(oh_all[:, blk], lg[:, 0], bc(ps_small[:, 9], E), ALU.is_equal))

            def post_weight(j, s):
                blk = bass.ds(j * GW, GW)
                dve.wait_ge(s_pe, add(j, 1))
                s(V.tensor_reduce(ps_small[:, 10], lg[:, 3], AX.X, ALU.add))
                s(V.reciprocal(ps_small[:, 11], ps_small[:, 10]))
                s(V.tensor_tensor(lgo[:], oh_all[:, blk], bc(ps_small[:, 11], E), ALU.mult))
                dve.sem_inc(s_ohp, 1)
                s(V.tensor_scalar(ohs_all[:, blk], lgo[:], wmax[0:ROWS, 6:7], None, ALU.mult))
                assert s.n == NPOST

            def sums(j, first):
                for p in range(NPAIR):
                    dve.wait_ge(s_exp, add(j * NPAIR, p + 1))
                    if p == 0:
                        if not first:
                            dve.wait_ge(s_pnum, j)
                        i = V.tensor_copy(esum[:], ex[:, 0])
                    else:
                        dve.wait_ge(s_es, add(j * NPAIR, p))
                        if p < LAST:
                            i = V.tensor_tensor(esum[:], esum[:], ex[:, p % NE], ALU.add)
                        else:
                            i = V.tensor_tensor(esum[0:KT_REST, 0], esum[0:KT_REST, 0],
                                                ex[0:KT_REST, p % NE, 0], ALU.add)
                    i.then_inc(s_es, 1)
                    if not first:
                        if p == 0:
                            s = post_steps(j - 1, 0)
                            post_norm(j - 1, s)
                        if p == 2:
                            post_center(j - 1, s)
                        if p == 4:
                            post_h2(j - 1, s)
                        if p == 10:
                            post_split(j - 1, s, 0)
                if not first:
                    post_route(j - 1, s)
                    return s

            NFIN = 13

            def combine(j, p):
                dve.wait_ge(s_l2, add(j * E, 2 * p + 4))
                if p == 0 and not (isinstance(j, int) and j == 0):
                    dve.wait_ge(pls, add((j - 1) * 13, 8))
                w = ohs_all[:, bass.ds(j * GW, GW), 2 * p:2 * p + 2]
                V.tensor_tensor(yt[:, p], pY[p % 2], bc(w), ALU.mult).then_inc(s_part, 1)

            def last_norm(s, src, k):
                s(V.tensor_reduce(fin_small[:, 6], src, AX.X, ALU.add))
                s(V.scalar_tensor_tensor(fin_t[:, k], bc(fin_small[:, 6]), -1.0 / D, src, ALU.mult, ALU.add))
                s(V.tensor_tensor(fin_t[:, 3], fin_t[:, k], fin_t[:, k], ALU.mult))
                s(V.tensor_reduce(fin_small[:, 7], fin_t[:, 3], AX.X, ALU.add))
                return V.tensor_scalar(fin_small[:, k], fin_small[:, 7], 1.0 / D, EPS, ALU.mult, ALU.add)

            def finish_center(j):
                s = Steps(dvf, j * NFIN)
                dve.wait_ge(s_ysum, add(j, 1))
                s(V.tensor_tensor(fin_t[:, 2].bitcast(I32), ya[:, 5].bitcast(I32), mask[:], ALU.bitwise_and))
                s(V.tensor_tensor(fin_t[:, 2], fin_t[:, 2], rest[:, 2], ALU.add))
                s(last_norm(s, fin_t[:, 2], 0))
                last_norm(s, h2_all[:, bass.ds(j * GW, GW)], 1).then_inc(s_froot_in, 1)
                return s

            def finish(j, s):
                blk = bass.ds(j * GW, GW)
                dve.wait_ge(s_froot, add(j, 1))
                s(V.tensor_tensor(ok_all[:, blk], fin_t[:, 0], bc(fin_small[:, 2]), ALU.mult))
                s(V.tensor_tensor(od_all[:, blk], fin_t[:, 1], bc(fin_small[:, 3]), ALU.mult))
                assert s.n == NFIN

            step(V.memset(ones_run[:], 1.0))

            sums(0, True)
            s = sums(1, False)
            post_weight(0, s)
            for p in range(4):
                combine(0, p)
            with dve.Fori(2, NB - 1) as j:
                s = sums(j, False)
                post_weight(j - 1, s)
                f = finish_center(j - 2)
                combine(j - 1, 0)
                combine(j - 1, 1)
                finish(j - 2, f)
                combine(j - 1, 2)
                combine(j - 1, 3)
            last = NB - 1
            s = sums(last, False)
            post_weight(last - 1, s)
            f = finish_center(last - 2)
            combine(last - 1, 0)
            finish(last - 2, f)
            combine(last - 1, 1)
            s = post_steps(last, 0)
            post_norm(last, s)
            post_center(last, s)
            combine(last - 1, 2)
            post_h2(last, s)
            combine(last - 1, 3)
            post_split(last, s, 1)
            post_route(last, s)
            post_weight(last, s)

            step(V.tensor_copy(ohe[:], oh_all[:].rearrange("p w e -> p e w")))
            step(V.tensor_reduce(rk_small[:, 0], ohe[:], AX.X, ALU.add))
            dve.sem_inc(s_cnt_in, 1)
            step(V.tensor_tensor_scan(pre[:].rearrange("p e w -> p (e w)"), ones_run[:],
                                      ohe[:].rearrange("p e w -> p (e w)"), 0.0, ALU.mult, ALU.add))
            combine(last, 0)
            f = finish_center(last - 1)
            finish(last - 1, f)
            dve.wait_ge(s_cnt, 1)
            step(V.tensor_copy(rk_small[:, 1:3].rearrange("p a e -> p (a e)"), pM[0:ROWS, 0:2 * E]))
            step(V.tensor_tensor(rk_small[:, 1, 1:E], rk_small[:, 1, 1:E], pre[:, 0:E - 1, W - 1], ALU.subtract))
            step(V.tensor_tensor(rk[:, 0], pre[:].rearrange("p e w -> p w e"), rows(rk_small[:, 1], W), ALU.add))
            step(V.tensor_tensor(rk[:, 1], rk[:, 0], oh_all[:], ALU.mult))
            step(V.tensor_reduce(rkw[:, 0], rk[:, 1], AX.X, ALU.add))
            step(V.tensor_tensor(rk[:, 2], oh_all[:], rows(rk_small[:, 2], W), ALU.mult))
            step(V.tensor_reduce(rkw[:, 1], rk[:, 2], AX.X, ALU.add))
            for c in range(COPIES):
                step(V.scalar_tensor_tensor(rkw[:, 2], rkw[:, 1], float(c), rkw[:, 0], ALU.mult, ALU.add))
                step(V.tensor_scalar(kept[:, c], rkw[:, 2], float(CAP), None, ALU.is_le))

            def choose(c, q):
                step(V.tensor_copy(o_all[:, c, q], od_all[:, q]))
                V.copy_predicated(o_all[:, c, q], bc(kept[:, c, q].bitcast(U32)), ok_all[:, q]).then_inc(s_out, 1)

            ahead = slice(0, LASTW)
            for c in range(COPIES):
                combine(last, c + 1)
                choose(c, ahead)
            finish(last, finish_center(last))
            for c in range(COPIES):
                choose(c, slice(LASTW, W))


def kernel(**inputs):
    import concourse.bacc as bacc
    from concourse.bass_utils import run_bass_kernel_spmd as run

    nc = bacc.Bacc("TRN2", target_bir_lowering=False, num_devices=1)
    arrays = {"in_packed": pack(inputs)}
    arrays.update({f"in_{n}": np.ascontiguousarray(inputs[n]) for n in ("x", "L0_ffn_w1", "L0_ffn_w2")})
    args = [nc.dram_tensor(n, a.shape, mybir.dt.from_np(a.dtype), kind="ExternalInput").ap()
            for n, a in arrays.items()]
    out = nc.dram_tensor("out_h", (B, COPIES * HP * W, D), F32, kind="ExternalOutput").ap()
    vit_layer(nc, *args, out)
    r = run(nc, [arrays], core_ids=[0])
    return r.results[0]["out_h"]
```

```python
from contextlib import ExitStack

import numpy as np

import concourse.bass as bass
from concourse import mybir

F32 = mybir.dt.float32
F16 = mybir.dt.float16
U32 = mybir.dt.uint32
I32 = mybir.dt.int32
ACT = mybir.ActivationFunctionType
ALU = mybir.AluOpType
AX = mybir.AxisListType

B, CH, IMG, PATCH = 4, 3, 224, 8
HP = IMG // PATCH
ROWS = B * HP
W = HP
D = 64
D2 = 2 * D
PD = CH * PATCH * PATCH
HALF = PD // 2
GW = 4
NB = W // GW
BLK = GW * ROWS
T = ROWS * W
COPIES = 3
E = 8
F = 256
FC = F // 128
CAP = -(-5 * COPIES * T // (4 * E))
KT_FULL = T // 128
KT_REST = T - KT_FULL * 128
KT = KT_FULL + 1
NPAIR = KT_FULL // 2 + 1
LAST = NPAIR - 1
PARTS = [slice(0, (NB - 2) * GW), slice((NB - 2) * GW, W)]
PAIRS = [slice(w, min(w + 2 * GW, W)) for w in range(0, W, 2 * GW)]
EPS = 1e-5
NORM_EPS = 1e-12
BIG = 3.4028234663852886e38
INF_AS = 10000.0
SPLIT = 256.0
WTOP = 8192.0


ACT_WP, DVE_LAST = (2, 3), 1
GROUPS = [range(4), range(4, NB)]
TR_BANK = [0, 2, 0, 2, 2, 2, 0]
SUM_BANK = [3, 2]
H_BANK = [(0, 1, 3)[g % 3] for g in range(NB)]
F_BANK = [0, 1, 0, 1, 2, 3, 0]


def layout():
    at, n = {}, 0
    for name, width in (("ident", 128), ("stack", D), ("base", ROWS), ("image", ROWS), ("ramp", E), ("centre", D2),
                        ("pair", 2), ("w1t", 2 * 2 * D), ("g1", 2), ("bl1", 2), ("b1", 1), ("wp1", D), ("g2", 1),
                        ("gp", 1), ("bp", 1), ("wp2", D2), ("bl2", ROWS), ("bp1", D), ("bp2", D), ("gate_b", E),
                        ("gate_w", E), ("eb1", E * FC), ("b2", E // 2)):
        at[name] = slice(n, n + width)
        n += width
    return at, n


AT, PACKED = layout()


def pack(v):
    c = np.zeros((128, PACKED), np.float32)

    def put(name, a):
        c[:a.shape[0], AT[name]] = a.reshape(a.shape[0], -1)

    put("ident", np.eye(128))
    put("stack", np.tile(np.eye(D), (2, 1)))
    b, hp = np.divmod(np.arange(ROWS), HP)
    put("base", COPIES * (b[:, None] < b[None, :]) + (b[:, None] == b[None, :]) * (hp[:, None] < hp[None, :]))
    put("image", b[:, None] == b[None, :])
    put("ramp", np.tile(E - np.arange(E), (128, 1)))
    halves = np.kron(np.eye(2), np.ones((D, D)))
    put("centre", np.eye(D2) - halves / D)
    put("pair", halves[:, [0, D]])

    def twice(a):
        return np.concatenate([a, a])

    def image_order(a):
        return a.reshape(PATCH * PATCH, CH, -1).transpose(1, 0, 2).reshape(2, HALF, -1).transpose(1, 0, 2)

    w = image_order(v["L0_tok_W1"])
    put("w1t", np.stack([w, w], 2))
    put("g1", image_order(v["L0_tok_ln1_g"]))
    put("bl1", image_order(v["L0_tok_ln1_b"]))
    for name, key in (("b1", "tok_b1"), ("g2", "tok_ln2_g"), ("gp", "tok_lnp_g"), ("bp", "tok_lnp_b"), ("wp1", "tok_Wp1")):
        put(name, twice(v["L0_" + key].reshape(D, -1)))
    wp2 = np.zeros((2, D, 2, D), np.float32)
    wp2[0, :, 0] = wp2[1, :, 1] = v["L0_tok_Wp2"]
    put("wp2", wp2.reshape(D2, D2))
    put("bl2", np.tile(v["L0_tok_ln2_b"][:, None], (1, ROWS)))
    for name, key in (("bp1", "tok_bp1"), ("bp2", "tok_bp2"), ("gate_b", "ffn_gate_b")):
        put(name, np.tile(v["L0_" + key], (128, 1)))
    put("gate_w", v["L0_ffn_gate_w"])
    put("eb1", v["L0_ffn_b1"].reshape(E * FC, 128).T)
    put("b2", v["L0_ffn_b2"].reshape(E // 2, D2).T)
    return c


def selectors():
    s = np.zeros((E, E // 2, 2, D), np.float16)
    for e in range(E):
        s[e, e // 2, e % 2] = 1.0
    return s.reshape(E, E // 2 * D2)


def add(n, k):
    return n + k if k else n


def vit_layer(nc, packed, select, x, w1, w2, out):
    with ExitStack() as ctx:
        def sb(name, shape, dt=F32):
            return ctx.enter_context(nc.sbuf_tensor(name, shape, dt))

        def sem(name):
            return ctx.enter_context(nc.semaphore(name))

        pk = sb("pk", [128, PACKED])

        def packed_at(name, n=128):
            return pk[0:n, AT[name]]

        ident = packed_at("ident")
        w1t = packed_at("w1t", HALF).rearrange("p (c k d) -> p c k d", c=2, k=2)
        sel = sb("sel", [E, E // 2 * D2], F16)
        img = sb("img", [ROWS, CH * PATCH, W, PATCH])
        xn = sb("xn", [ROWS, W, PD])
        xt = sb("xt", [HALF, 2, 2, BLK])
        stats = sb("stats", [ROWS, W, 6])
        ones_col = sb("ones_col", [128, 1])
        half_neg = sb("half_neg", [ROWS, W])
        w1g = sb("w1g", [HALF, 2, D])
        wp1g = sb("wp1g", [D2, D])
        wp1d = sb("wp1d", [D2, 2, D])
        wp2h = sb("wp2h", [D2, D2])
        b1c = sb("b1c", [D2, 2])
        bias2 = sb("bias2", [ROWS, D])
        cen = sb("cen", [128, 8])
        ew1 = sb("ew1", [128, E, F])
        ew1s = sb("ew1s", [128, E, F])
        ew1h = sb("ew1h", [128, E, F], F16)
        ew1l = sb("ew1l", [128, E, F], F16)
        ew2 = sb("ew2", [128, E * FC, D])
        eb1s = sb("eb1s", [128, E * FC])
        wmax = sb("wmax", [128, 8])
        room = sb("room", [ROWS, 3 * W * D])

        def part(at, *shape):
            n, axes = 1, " ".join(f"a{i}" for i in range(len(shape)))
            for k in shape:
                n *= k
            return room[:, at:at + n].rearrange(f"p ({axes}) -> p {axes}", **{f"a{i}": k for i, k in enumerate(shape)})

        ta, tb, tc = (part(k * W * D, W, D) for k in range(3))
        h_all = sb("h_all", [ROWS, W, D])
        f_all = sb("f_all", [ROWS, W, D])
        fdup = img[:].rearrange("p q w r -> p (q w r)")[:, 0:W * 2 * D].rearrange("p (w a d) -> p w a d", a=2, d=D)
        small = sb("small", [ROWS, 12, W])
        fT = xn[0:D].rearrange("p w f -> p (w f)")[:, 0:T]
        QH = sb("QH", [128, T], F16)
        QL = sb("QL", [128, T], F16)
        KHL = sb("KHL", [128, KT * 128], F16)

        def before(ap, at, n):
            k = at * 2 * ROWS
            return ap[:].bitcast(F32)[:, k:k + n * 2 * ROWS].rearrange("p (n t) -> p n t", n=n)

        ucols = before(QH, 0, NB)
        zc = before(QL, 0, 2)
        th = before(QL, 2, 2)
        sc = before(QL, 4, 2)
        usq = before(KHL, 0, 2)
        f2 = sb("f2", [128, KT_FULL + 1, D])
        NE = 4
        ex = sb("ex", [128, NE, 2, BLK])
        esum = sb("esum", [128, 2, BLK])
        att = sb("att", [128, BLK])
        h2row = sb("h2row", [ROWS, GW, D])
        h2dup = sb("h2dup", [ROWS, GW, 2, D])
        xcol = sb("xcol", [128, BLK])
        xhl = sb("xhl", [128, 2, BLK], F16)
        lg = sb("lg", [ROWS, 4, GW, E])
        hot = sb("hot", [ROWS, GW, E])
        ones_run = sb("ones_run", [ROWS, E * W])
        ps_small = sb("ps_small", [ROWS, 12, GW])
        hotT = sb("hotT", [E, BLK], F16)
        msk = sb("msk", [128, E // 2, BLK], F16)
        b2s = sb("b2s", [128, E // 2])
        yacc = sb("yacc", [128, BLK])
        ynew = sb("ynew", [128, BLK])
        oh_all = sb("oh_all", [ROWS, W, E])
        h2_all = sb("h2_all", [ROWS, W, D])
        hm = [ew1s[:].rearrange("p e f -> p (e f)")[:, 0:4 * BLK].rearrange("p (n t) -> p n t", n=4),
              ex[:, 1:3].rearrange("p s k t -> p (s k) t")]
        y_row = part(0, GW, D)
        y_zero = part(GW * D, GW, D)
        pt = part(14 * GW * D, 4, GW, D)
        rest = part(18 * GW * D, 3, GW, D)
        zeros = sb("zeros", [ROWS, GW, D])
        mask = sb("mask", [ROWS, GW, D], I32)
        fin_small = sb("fin_small", [ROWS, 8, GW])
        fin_t = sb("fin_t", [ROWS, 4, GW, D])
        outcomes = img[:].rearrange("p q w r -> p (q w r)").rearrange("p (k w d) -> p k w d", k=3, d=D)
        ok_all, od_all = outcomes[:, 0], outcomes[:, 1]
        weight = sb("weight", [ROWS, GW])
        ohe = sb("ohe", [ROWS, E, W])
        pre = sb("pre", [ROWS, E, W])
        rk = sb("rk", [ROWS, 3, W, E])
        rk_small = sb("rk_small", [ROWS, 4, E])
        kept = sb("kept", [ROWS, COPIES, W])
        rkw = sb("rkw", [ROWS, 3, W])
        o_all = xn[:].rearrange("p w f -> p (w f)").rearrange("p (c w d) -> p c w d", c=COPIES, d=D)

        pS = ctx.enter_context(nc.psum_tensor("pS", [128, 4, 512], F32))
        pR = ctx.enter_context(nc.psum_tensor("pR", [128, 4, 512], F32))
        pAV = pR[:, 0, 0:BLK]
        pY = [pR[:, 1 + i, 0:BLK] for i in range(2)]
        pM = pR[:, 3, :]
        pA = pM[0:ROWS, 0:GW * D].rearrange("p (w d) -> p w d", d=D)
        pDen = pM[0:ROWS, GW * D:GW * D + GW]
        pHot = pR[0:E, 0, 0:BLK]
        pLog = pM[0:ROWS, 0:GW * E].rearrange("p (w e) -> p w e", e=E)

        ld_img, ld_pack, ld_w1, ld_w2 = (sem(n) for n in ("ld_img", "ld_pack", "ld_w1", "ld_w2"))
        zeroed = sem("zeroed")
        dv = sem("dv")
        dvp = sem("dvp")
        dvc = sem("dvc")
        dvf = sem("dvf")
        s_proot_in, s_proot = sem("s_proot_in"), sem("s_proot")
        s_froot_in, s_froot = sem("s_froot_in"), sem("s_froot")
        s_wts = sem("s_wts")
        s_wp2 = sem("s_wp2")
        s_bias = sem("s_bias")
        s_b1 = sem("s_b1")
        s_b1c = sem("s_b1c")
        s_biasc = sem("s_biasc")
        s_wmax_in, s_wmax = sem("s_wmax_in"), sem("s_wmax")
        s_wscale = sem("s_wscale")
        s_wcut = sem("s_wcut")
        s_ln1 = sem("s_ln1")
        s_xn = sem("s_xn")
        s_xa = sem("s_xa")
        s_tr = sem("s_tr")
        s_trc = sem("s_trc")
        s_mm = sem("s_mm")
        s_u = sem("s_u")
        s_ssq = sem("s_ssq")
        s_mm1 = sem("s_mm1")
        s_p = sem("s_p")
        s_sq = sem("s_sq")
        s_z = sem("s_z")
        s_zt = sem("s_zt")
        s_zc = sem("s_zc")
        s_sc = sem("s_sc")
        s_mm2 = sem("s_mm2")
        s_h = sem("s_h")
        s_hsq = sem("s_hsq")
        s_f = sem("s_f")
        s_fd = sem("s_fd")
        s_ft = sem("s_ft")
        s_ftc = sem("s_ftc")
        s_ql = sem("s_ql")
        s_khl = sem("s_khl")
        s_f2 = sem("s_f2")
        s_f2c = sem("s_f2c")
        s_S = sem("s_S")
        s_exp = sem("s_exp")
        s_es = sem("s_es")
        s_den = sem("s_den")
        s_av = sem("s_av")
        s_att = sem("s_att")
        s_pnum = sem("s_pnum")
        s_pt = sem("s_pt")
        s_psq = sem("s_psq")
        s_h2 = sem("s_h2")
        s_h2d = sem("s_h2d")
        s_h2t = sem("s_h2t")
        s_xh = sem("s_xh")
        s_x16 = sem("s_x16")
        s_log = sem("s_log")
        s_lm = sem("s_lm")
        s_pe = sem("s_pe")
        s_hot = sem("s_hot")
        s_turn = sem("s_turn")
        s_hott = sem("s_hott")
        s_mask = sem("s_mask")
        s_mskc = sem("s_mskc")
        s_l1 = sem("s_l1")
        s_relu = sem("s_relu")
        s_l2 = sem("s_l2")
        s_part = sem("s_part")
        s_yb = sem("s_yb")
        s_y = sem("s_y")
        s_ysum = sem("s_ysum")
        pls = sem("pls")
        s_cnt_in, s_cnt = sem("s_cnt_in"), sem("s_cnt")
        s_cntc = sem("s_cntc")
        s_od = sem("s_od")
        s_oc = sem("s_oc")
        s_out = sem("s_out")
        st_out = sem("st_out")

        ctx.enter_context(nc.allow_non_contiguous_dma(reason="a few hundred gains and biases, one to a partition"))
        block = ctx.enter_context(nc.Block())

        img_src = x.rearrange("b c (h q) w -> b h c (q w)", q=PATCH)

        def load_image(eng, b):
            for c in range(CH):
                dst = img[b * HP:(b + 1) * HP, c * PATCH:(c + 1) * PATCH].rearrange("p q w r -> p (q w r)")
                eng.dma_start(dst, img_src[b, :, c]).then_inc(ld_img, 16)

        @block.sync
        def _(sp):
            for b in (0, 1, 2, 3):
                load_image(sp, b)
            for half in range(2):
                sp.dma_start(ew1[half * D:(half + 1) * D], w1.rearrange("e d f -> d e f")).then_inc(ld_w1, 16)
            sp.dma_start(ew2[:], w2.rearrange("e (c p) d -> p (e c) d", p=128)).then_inc(ld_w2, 16)
            for n, part_w in enumerate(PARTS):
                w0, w1_ = part_w.start, part_w.stop
                for c in range(COPIES):
                    sp.wait_ge(s_out, n * COPIES + c + 1)
                    for b in range(B):
                        dst = out[b].rearrange("(c h w) d -> c h (w d)", c=COPIES, h=HP)[c]
                        src = o_all[b * HP:(b + 1) * HP, c, w0:w1_].rearrange("p w d -> p (w d)")
                        sp.dma_start(dst[:, w0 * D:w1_ * D], src).then_inc(st_out, 16)
            sp.wait_ge(st_out, 2 * 16 * COPIES * B)

        @block.gpsimd
        def _(pool):
            nc.gpsimd.memset(half_neg[:], -0.5).then_inc(zeroed, 1)
            nc.gpsimd.memset(ones_col[:], 1.0).then_inc(zeroed, 1)
            nc.gpsimd.memset(wp1d[:], 0.0).then_inc(zeroed, 1)
            nc.gpsimd.memset(KHL[:, T:KT * 128], 0.0).then_inc(zeroed, 1)
            pool.wait_ge(zeroed, 4)
            nc.gpsimd.memset(f2[KT_REST:128, KT_FULL], 0.0).then_inc(zeroed, 1)
            pool.wait_ge(zeroed, 5)
            nc.gpsimd.memset(zeros[:], 0.0).then_inc(zeroed, 1)
            pool.wait_ge(s_wmax_in, 1)
            nc.gpsimd.partition_all_reduce(wmax[:, 1:2], wmax[:, 0:1], 128,
                                           bass.bass_isa.ReduceOp.max).then_inc(s_wmax, 1)

            pool.wait_ge(s_wscale, 1)
            nc.gpsimd.tensor_scalar(ew1s[:], ew1[:], wmax[:, 4:5], None, ALU.mult).then_inc(s_wcut, 1)
            pool.wait_ge(s_wcut, 1)
            nc.gpsimd.tensor_copy(ew1h[:], ew1s[:]).then_inc(s_wcut, 1)
            pool.wait_ge(s_wcut, 2)
            nc.gpsimd.tensor_tensor(ew1l[:], ew1s[:], ew1h[:], ALU.subtract).then_inc(s_wcut, 1)

            def roots(n, src, dst, sin, sout):
                pool.wait_ge(sin, add(n, 1))
                nc.gpsimd.tensor_tensor(dst, src, half_neg[:, 0:GW], ALU.pow).then_inc(sout, 1)

            def post(j):
                roots(2 * j, ps_small[:, 1], ps_small[:, 2], s_proot_in, s_proot)
                roots(2 * j + 1, ps_small[:, 4], ps_small[:, 5], s_proot_in, s_proot)
                pool.wait_ge(s_proot, add(j * 2, 2))
                if not (isinstance(j, int) and j == 0):
                    pool.wait_ge(s_h2d, j * 2)
                r = ps_small[:, 5].unsqueeze(2).broadcast_to([ROWS, GW, D])
                nc.gpsimd.tensor_tensor(h2row[:], pt[:, 2], r, ALU.mult).then_inc(s_h2, 1)

            def finite(j):
                base = j * 5
                pool.wait_ge(s_y, add(j, 1))
                nc.gpsimd.tensor_tensor(y_zero, y_row, zeros[:], ALU.mult).then_inc(pls, 1)
                nc.gpsimd.tensor_scalar(rest[:, 0], y_row, BIG, INF_AS, ALU.is_gt, ALU.mult).then_inc(pls, 1)
                nc.gpsimd.tensor_scalar(rest[:, 1], y_row, -BIG, -INF_AS, ALU.is_lt, ALU.mult).then_inc(pls, 1)
                pool.wait_ge(pls, add(base, 3))
                nc.gpsimd.tensor_tensor(rest[:, 0], rest[:, 0], rest[:, 1], ALU.add).then_inc(pls, 1)
                nc.gpsimd.tensor_scalar(mask[:], y_zero, 0.0, -1.0, ALU.is_equal, ALU.mult).then_inc(pls, 1)
                pool.wait_ge(pls, add(base, 5))
                nc.gpsimd.tensor_tensor(rest[:, 2], rest[:, 0], h2_all[:, bass.ds(j * GW, GW)], ALU.add).then_inc(s_ysum, 1)

            def last_roots(j):
                pool.wait_ge(s_froot_in, add(j, 1))
                nc.gpsimd.tensor_tensor(fin_small[:, 2:4], fin_small[:, 0:2],
                                        half_neg[:, 0:2 * GW].rearrange("p (k w) -> p k w", k=2),
                                        ALU.pow).then_inc(s_froot, 1)

            def stage(j):
                post(j - 1)
                finite(j - 2)
                last_roots(j - 2)

            post(0)
            with pool.Fori(2, NB - 1) as j:
                stage(j)
            post(NB - 2)
            finite(NB - 3)
            post(NB - 1)
            finite(NB - 2)
            last_roots(NB - 3)
            last_roots(NB - 2)
            finite(NB - 1)
            last_roots(NB - 1)

        @block.scalar
        def _(act):
            act.dma_start(pk[:], packed).then_inc(ld_pack, 16)
            act.dma_start(sel[:], select).then_inc(ld_w2, 16)
            act.wait_ge(ld_pack, 16)
            nc.scalar.mul(wp2h[:], packed_at("wp2"), 0.5).then_inc(s_wp2, 1)
            def copy_patches(g):
                act.wait_ge(s_tr, g + 1)
                if g >= 2:
                    act.wait_ge(s_mm, g - 1)
                b = TR_BANK[g]
                nc.scalar.copy(xt[:, g % 2], pS[0:HALF, b:b + 2, 0:BLK]).then_inc(s_trc, 1)

            def copy_tokens(g):
                if g == 0:
                    act.wait_ge(s_biasc, 1)
                act.wait_ge(s_mm, g + 1)
                u = pR[:, g % 2, 0:2 * ROWS]
                nc.scalar.activation(ucols[:, g], u, ACT.Identity, bias=b1c[:, 1:2]).then_inc(s_u, 1)
                if g >= 2:
                    act.wait_ge(s_ssq, g - 1)
                nc.scalar.activation(usq[:, g % 2], u, ACT.Square, bias=b1c[:, 1:2]).then_inc(s_u, 1)

            def square_pair(k):
                act.wait_ge(s_p, k + 1)
                nc.scalar.square(tb[:, PAIRS[k]], ta[:, PAIRS[k]]).then_inc(s_sq, 1)

            def silu(g):
                act.wait_ge(s_zt, g + 1)
                if g >= 2:
                    act.wait_ge(s_sc, g - 1)
                nc.scalar.activation(zc[:, g % 2], pS[:, 2 + g % 2, 0:2 * ROWS], ACT.Identity,
                                     bias=packed_at("bp"), scale=packed_at("gp")).then_inc(s_zc, 1)
                act.wait_ge(s_zc, 2 * g + 1)
                nc.scalar.activation(th[:, g % 2], zc[:, g % 2], ACT.Tanh, scale=0.5).then_inc(s_zc, 1)

            def square_h(g):
                act.wait_ge(s_h, g + 1)
                q = slice(g * GW, (g + 1) * GW)
                nc.scalar.square(tb[:, q], h_all[:, q]).then_inc(s_hsq, 1)

            def double(src):
                return src.unsqueeze(2).broadcast_to([ROWS, GW, 2, D])

            def double_f(g):
                act.wait_ge(s_f, g + 1)
                q = slice(g * GW, (g + 1) * GW)
                nc.scalar.copy(fdup[:, q], double(f_all[:, q])).then_inc(s_fd, 1)

            def copy_f(g):
                act.wait_ge(s_ft, g + 1)
                q = slice(g * BLK, (g + 1) * BLK)
                nc.scalar.copy(QH[:, q], pS[:, F_BANK[g], 0:BLK]).then_inc(s_ftc, 1)
                nc.scalar.copy(fT[:, q], pS[0:D, F_BANK[g], 0:BLK]).then_inc(s_ftc, 1)

            def copy_f2(k):
                act.wait_ge(s_f2, k + 1)
                n, m = (8, 128) if k < 3 else (1, KT_REST)
                nc.scalar.copy(f2[0:m, 8 * k:8 * k + n],
                               pR[0:m, k, 0:n * D].rearrange("p (n d) -> p n d", d=D)).then_inc(s_f2c, 1)

            def normalise(g):
                for w in ACT_WP:
                    w += g * GW
                    i = nc.scalar.activation(xn[:, w].rearrange("p (a r) -> p a r", r=PATCH), img[:, :, w, :], ACT.Identity,
                                             bias=small[:, 6, w:w + 1], scale=small[:, 1, w:w + 1])
                i.then_inc(s_xa, 1)

            act.wait_ge(s_ln1, 1)
            for g in (0, 1, 2):
                normalise(g)
            copy_patches(0)
            normalise(3)
            for g in (1, 2):
                copy_patches(g)
                copy_tokens(g - 1)
            copy_patches(3)
            copy_tokens(2)
            act.wait_ge(s_ln1, 2)
            normalise(4)
            copy_tokens(3)
            normalise(5)
            normalise(6)
            copy_patches(4)
            copy_patches(5)
            copy_tokens(4)
            square_pair(0)
            square_pair(1)
            copy_patches(6)
            copy_tokens(5)
            copy_tokens(6)
            silu(0)
            silu(1)
            square_pair(2)
            silu(2)
            square_pair(3)
            silu(3)
            for g in GROUPS[0]:
                square_h(g)
            silu(4)
            silu(5)
            double_f(0)
            double_f(1)
            silu(6)
            double_f(2)
            double_f(3)
            for g in GROUPS[1]:
                square_h(g)
            for g in (0, 1):
                copy_f(g)
            double_f(4)
            for g in (2, 3):
                copy_f(g)
            copy_f2(0)
            double_f(5)
            copy_f(4)
            double_f(6)
            copy_f(5)
            copy_f2(1)
            copy_f(6)
            copy_f2(2)
            copy_f2(3)

            def exponentials(j, first, after_experts=True):
                for p in range(NPAIR):
                    act.wait_ge(s_S, add(j * NPAIR, p + 1))
                    if not (first and p < NE):
                        act.wait_ge(s_av, add(j * NPAIR, max(p + 1 - NE, 0)))
                        act.wait_ge(s_es, add(j * NPAIR, max(p + 1 - NE, 0)))
                    if p == 1 and not first and after_experts:
                        act.wait_ge(s_l2, add(j * 4, -2))
                    if p < LAST:
                        o, i = ex[:, p % NE], pS[:, 2 * (p % 2):2 * (p % 2) + 2, 0:BLK]
                    else:
                        o, i = ex[:, p % NE, 0], pS[:, 2 * (p % 2), 0:BLK]
                    nc.scalar.activation(o, i, ACT.Exp, scale=1.0 / (SPLIT * SPLIT)).then_inc(s_exp, 1)
                    if p == 1 and not first:
                        square_rows(2 * (j - 1), 1)
                    if p == 4 and not first:
                        square_rows(2 * (j - 1) + 1, 2)
                    if p == 7 and not first:
                        keep_h2(j - 1)
                    if p == 9 and not first:
                        copy_columns(j - 1, 0)
                act.wait_ge(s_av, add(j * NPAIR, NPAIR))
                if not first:
                    act.wait_ge(s_pnum, j)
                nc.scalar.copy(att[:], pAV).then_inc(s_att, 1)

            def square_rows(n, k):
                act.wait_ge(s_pt, add(n, 1))
                nc.scalar.square(pt[:, 3], pt[:, k]).then_inc(s_psq, 1)

            def keep_h2(j):
                act.wait_ge(s_h2, add(j, 1))
                nc.scalar.copy(h2dup[:], double(h2row[:])).then_inc(s_h2d, 1)
                nc.scalar.copy(h2_all[:, bass.ds(j * GW, GW)], h2row[:]).then_inc(s_h2d, 1)

            def copy_columns(j, slot):
                act.wait_ge(s_h2t, add(j, 1))
                nc.scalar.copy(xcol[:], pM[:, 0:BLK]).then_inc(s_xh, 1)
                nc.scalar.activation(xhl[:, slot], pM[:, 0:BLK], ACT.Copy, scale=SPLIT).then_inc(s_xh, 1)

            def gate_exp(j):
                act.wait_ge(s_lm, add(j, 1))
                nc.scalar.activation(lg[:, 3], lg[:, 2], ACT.Exp).then_inc(s_pe, 1)

            def copy_mask(j, p):
                act.wait_ge(s_mask, add(j * 4, p + 1))
                if not (isinstance(j, int) and j == 0):
                    act.wait_ge(s_part, add(j * 4, p - 1))
                nc.scalar.copy(msk[:, p], pAV).then_inc(s_mskc, 1)

            def relus(j, slot=0, last_post=False):
                for p in range(4):
                    if p == 1:
                        act.wait_ge(s_es, NPAIR * NB if slot else add(j * NPAIR, 2 * NPAIR))
                    for i in range(4):
                        e, k = 2 * p + i % 2, i // 2
                        act.wait_ge(s_l1, add(j * E * FC, 4 * p + i + 1))
                        act.wait_ge(s_l2, add(j * 4, p + 1))
                        nc.scalar.activation(hm[p % 2][:, i], pS[:, i, 0:BLK], ACT.Relu,
                                             bias=eb1s[:, FC * e + k:FC * e + k + 1]).then_inc(s_relu, 1)
                        if p == 0 and i == 1:
                            gate_exp(j)
                    if p == 0:
                        act.wait_ge(s_turn, add(j, 1))
                        nc.scalar.copy(hotT[:], pHot).then_inc(s_hott, 1)
                    elif p < 3 or not last_post:
                        copy_mask(j, p - 1)
                    if p == 2 and last_post:
                        copy_mask(j, p)
                    if p == 3:
                        if last_post:
                            keep_h2(NB - 1)
                        copy_mask(j, 3)
                if last_post:
                    copy_columns(NB - 1, 1)

            exponentials(0, True)
            exponentials(1, False, after_experts=False)
            act.wait_ge(s_wscale, 1)
            relus(0)
            with act.Fori(2, NB - 1) as j:
                exponentials(j, False)
                relus(j - 1)
            exponentials(NB - 1, False)
            relus(NB - 2, last_post=True)
            relus(NB - 1, slot=1)
            for n, q in enumerate(PARTS):
                act.wait_ge(s_od, n + 1)
                for c in range(COPIES):
                    nc.scalar.copy(o_all[:, c, q], od_all[:, q]).then_inc(s_oc, 1)

        @block.tensor
        def _(pe):
            MM = pe.matmul
            pe.sem_inc(s_l2, 2)
            pe.wait_ge(ld_pack, 16)
            for c in range(2):
                MM(pR[:, 3, 64:65], w1t[:, c].rearrange("p k d -> p (k d)"), packed_at("bl1", HALF)[:, c:c + 1],
                   start=(c == 0), stop=(c == 1))
            MM(pR[0:ROWS, 3, 128:128 + D], packed_at("bl2", D), packed_at("wp1", D),
               start=True, stop=True).then_inc(s_bias, 1)
            pe.wait_ge(s_b1, 1)
            MM(pR[:, 3, 65:66], packed_at("centre"), b1c[:, 0:1], start=True, stop=True).then_inc(s_b1c, 1)

            def tokenize(g):
                pe.wait_ge(s_xn, g + 1)
                pe.wait_ge(s_xa, g + 1)
                if g == 6:
                    pe.wait_ge(s_p, 2)
                elif g >= 2:
                    pe.wait_ge(s_trc, {2: 1, 3: 2, 4: 4, 5: 5}[g])
                for w in range(GW):
                    for c in range(2):
                        i = pe.transpose(pS[0:HALF, TR_BANK[g] + c, w * ROWS:(w + 1) * ROWS],
                                         xn[:, g * GW + w, c * HALF:(c + 1) * HALF], ident[0:ROWS, 0:ROWS])
                i.then_inc(s_tr, 1)

            def project(g):
                pe.wait_ge(s_trc, g + 1)
                if g == 0:
                    pe.wait_ge(s_wts, 1)
                if g >= 2:
                    pe.wait_ge(s_u, 2 * (g - 1))
                for c in range(2):
                    x2 = xt[:, g % 2, c].rearrange("p (q h r) -> p h q r", q=2, h=2)
                    for h in range(2):
                        i = MM(pR[h * D:(h + 1) * D, g % 2, 0:2 * ROWS], w1g[:, c], x2[:, h],
                               start=(c == 0), stop=(c == 1))
                i.then_inc(s_mm, 1)

            def square_sums(g):
                pe.wait_ge(s_u, 2 * (g + 1))
                if g == 0:
                    pe.wait_ge(s_biasc, 1)
                for q in range(2):
                    w = g * GW + 2 * q
                    i = MM(pR[0:ROWS, SUM_BANK[g // 4], w:w + 2], usq[:, g % 2, q * ROWS:(q + 1) * ROWS],
                           packed_at("pair"), start=True, stop=True)
                i.then_inc(s_ssq, 1)

            def second_product(group):
                pe.wait_ge(s_trc, group[-1] + 1)
                for g in group:
                    for q in range(2):
                        o = (g % 2) * GW * D + q * D2
                        i = MM(pS[0:ROWS, (g - group[0]) // 2, o:o + D2], ucols[:, g, q * ROWS:(q + 1) * ROWS],
                               wp1d[:].rearrange("p h d -> p (h d)"), start=True, stop=True)
                i.then_inc(s_mm1, 1)

            def turn_z(g):
                pe.wait_ge(s_z, g // 2 + 1)
                if g >= 2:
                    pe.wait_ge(s_zc, 2 * (g - 2) + 1)
                for q in range(2):
                    w = g * GW + 2 * q
                    i = pe.transpose(pS[:, 2 + g % 2, q * ROWS:(q + 1) * ROWS],
                                     tc[:, w:w + 2].rearrange("p w d -> p (w d)"), ident[0:ROWS, 0:ROWS])
                i.then_inc(s_zt, 1)

            def third_product(g):
                pe.wait_ge(s_sc, g + 1)
                if g >= 3:
                    pe.wait_ge(s_h, g - 2)
                for q in range(2):
                    i = MM(pR[0:ROWS, H_BANK[g], q * D2:(q + 1) * D2], sc[:, g % 2, q * ROWS:(q + 1) * ROWS], wp2h[:],
                           start=True, stop=True)
                i.then_inc(s_mm2, 1)

            def turn_f(g):
                pe.wait_ge(s_fd, g + 1)
                if g < 2:
                    pe.wait_ge(s_p, 4)
                elif F_BANK[g] >= 2:
                    pe.wait_ge(s_zc, 2 * NB)
                else:
                    last_use = max(k for k in range(g) if F_BANK[k] == F_BANK[g])
                    pe.wait_ge(s_ftc, 2 * (last_use + 1))
                    pe.wait_ge(s_ql, last_use + 1)
                for w in range(GW):
                    i = pe.transpose(pS[:, F_BANK[g], w * ROWS:(w + 1) * ROWS],
                                     fdup[:, g * GW + w].rearrange("p a d -> p (a d)"), ident[0:ROWS, 0:ROWS])
                i.then_inc(s_ft, 1)

            for group in GROUPS:
                a, n = group[0], len(group)
                for i in range(n + 2):
                    if i < n:
                        tokenize(a + i)
                    if 1 <= i <= n:
                        project(a + i - 1)
                    if i >= 2:
                        square_sums(a + i - 2)
                second_product(group)
            pe.wait_ge(s_wp2, 1)
            for group in GROUPS:
                a, n = group[0], len(group)
                for i in range(n + 1):
                    if i < n:
                        turn_z(a + i)
                    if i:
                        third_product(a + i - 1)

            def back_to_rows(k):
                pe.wait_ge(s_ftc, 2 * min(-(-1024 * (k + 1) // BLK), NB))
                for n in range(8 * k, min(8 * k + 8, KT)):
                    m = 128 if n < KT_FULL else KT_REST
                    i = pe.transpose(pR[0:m, k, (n % 8) * D:(n % 8 + 1) * D], fT[:, n * 128:n * 128 + m],
                                     ident[0:D, 0:D])
                i.then_inc(s_f2, 1)

            for g in (0, 1, 2, 3):
                turn_f(g)
            pe.wait_ge(s_h, NB)
            back_to_rows(0)
            turn_f(4)
            turn_f(5)
            back_to_rows(1)
            turn_f(6)

            def scores(j, first, p):
                if p < 2:
                    if not first:
                        pe.wait_ge(s_exp, j * NPAIR)
                else:
                    pe.wait_ge(s_exp, add(j * NPAIR, p - 1))
                tiles = 2 if p < LAST else 1
                for t in range(tiles):
                    k0 = (2 * p + t) * 128
                    o = pS[:, 2 * (p % 2) + t, 0:BLK]
                    MM(o, KHL[:, k0:k0 + 128], QH[:, bass.ds(j * BLK, BLK)], start=True, stop=False)
                    i = MM(o, KHL[:, k0:k0 + 128], QL[:, bass.ds(j * BLK, BLK)], start=False, stop=True)
                i.then_inc(s_S, 1)

            def values(j, first, second, p):
                pe.wait_ge(s_exp, add(j * NPAIR, p + 1))
                if p == 0 and not first:
                    pe.wait_ge(s_att, j)
                    if second:
                        pe.wait_ge(s_mskc, add(j * 4, -4))
                if p < LAST:
                    for t in range(2):
                        i = MM(pR[t * D:(t + 1) * D, 0, 0:BLK], f2[:, 2 * p + t], ex[:, p % NE, t],
                               start=(p == 0), stop=(p == LAST - t))
                else:
                    i = MM(pR[0:D, 0, 0:BLK], f2[:, 2 * p], ex[:, p % NE, 0],
                           start=False, stop=True)
                i.then_inc(s_av, 1)

            def post_sums(j):
                pe.wait_ge(s_den, add(j, 1))
                pe.wait_ge(s_att, add(j, 1))
                if not (isinstance(j, int) and j == 0):
                    pe.wait_ge(s_lm, j)
                for w in range(GW):
                    q = slice(w * ROWS, (w + 1) * ROWS)
                    MM(pDen[:, w:w + 1], esum[:, 0, q], ones_col[:], start=True, stop=True)
                for w in range(GW):
                    q = slice(w * ROWS, (w + 1) * ROWS)
                    i = MM(pA[:, w], att[:, q], packed_at("stack"), start=True, stop=True)
                i.then_inc(s_pnum, 1)

            def post_cols(j):
                pe.wait_ge(s_h2d, add(j * 2, 2))
                for w in range(GW):
                    i = pe.transpose(pM[:, w * ROWS:(w + 1) * ROWS], h2dup[:, w].rearrange("p a d -> p (a d)"),
                                     ident[0:ROWS, 0:ROWS])
                i.then_inc(s_h2t, 1)

            def post_gate(j):
                pe.wait_ge(s_x16, add(j, 1))
                for w in range(GW):
                    i = MM(pLog[:, w], xcol[:, w * ROWS:(w + 1) * ROWS], packed_at("gate_w"), start=True, stop=True)
                i.then_inc(s_log, 1)

            def post_turn(j):
                pe.wait_ge(s_hot, add(j, 1))
                for w in range(GW):
                    i = pe.transpose(pHot[:, w * ROWS:(w + 1) * ROWS], hot[:, w], ident[0:ROWS, 0:ROWS])
                i.then_inc(s_turn, 1)

            def expert_mask(j, p):
                pe.wait_ge(s_hott, add(j, 1))
                if p:
                    pe.wait_ge(s_mskc, add(j * 4, p))
                MM(pAV, sel[:, p * D2:(p + 1) * D2], hotT[:], start=True, stop=True).then_inc(s_mask, 1)

            def rows_back(j):
                pe.wait_ge(s_part, add(j * 4, 6))
                for w in range(GW):
                    i = MM(pA[:, w], yacc[:, w * ROWS:(w + 1) * ROWS], packed_at("stack"), start=True, stop=True)
                i.then_inc(s_yb, 1)

            def attention(j, first, second=True):
                for p in range(NPAIR + 1):
                    if p < NPAIR:
                        scores(j, first, p)
                    if p:
                        values(j, first, second, p - 1)
                    if first and p == 0:
                        back_to_rows(2)
                        back_to_rows(3)
                        pe.wait_ge(s_f2c, 4)
                    if not first:
                        if p == 0:
                            post_sums(j - 1)
                        if p == 4 and second:
                            pe.wait_ge(s_proot_in, add(j * 2, -1))
                            rows_back(j - 2)
                        if p == 8:
                            if second:
                                pe.wait_ge(s_y, add(j, -1))
                            post_cols(j - 1)
                        if p == NPAIR:
                            post_gate(j - 1)

            def hidden(j, p, slot):
                for i in range(4):
                    if p:
                        pe.wait_ge(s_relu, add(j * E * FC, 4 * p - 3 + i))
                    o = pS[:, i, 0:BLK]
                    e, k = 2 * p + i % 2, (i // 2) * 128
                    MM(o, ew1h[:, e, k:k + 128], xhl[:, slot], start=True, stop=False)
                    MM(o, ew1l[:, e, k:k + 128], xhl[:, slot], start=False, stop=True).then_inc(s_l1, 1)

            def outputs(j, p):
                pe.wait_ge(s_relu, add(j * E * FC, 4 * p + 4))
                pe.wait_ge(s_part, add(j * 4, p + 1))
                for i in range(4):
                    h, c = i % 2, i // 2
                    ins = MM(pR[h * D:(h + 1) * D, 1 + p % 2, 0:BLK], ew2[:, FC * (2 * p + h) + c],
                             hm[p % 2][:, i], start=(c == 0), stop=(c == FC - 1))
                ins.then_inc(s_l2, 1)

            def queue_bases():
                pe.wait_ge(s_y, NB - 1)
                pe.wait_ge(s_cnt_in, 1)
                MM(pM[0:ROWS, 0:E], packed_at("base", ROWS), rk_small[:, 0], start=True, stop=True)
                MM(pM[0:ROWS, E:2 * E], packed_at("image", ROWS), rk_small[:, 0],
                   start=True, stop=True).then_inc(s_cnt, 1)

            def experts(j, last_post=False, slot=0):
                last = slot == 1
                pe.wait_ge(s_exp, NPAIR * NB if last else add(j * NPAIR, 2 * NPAIR))
                if last:
                    pe.wait_ge(s_relu, j * E * FC)
                pe.wait_ge(s_x16, add(j, 1))
                hidden(j, 0, slot)
                if last_post:
                    post_sums(NB - 1)
                if last:
                    pe.wait_ge(s_lm, NB)
                    rows_back(NB - 2)
                pe.wait_ge(s_att, NB if last else add(j, 2))
                if last:
                    pe.wait_ge(s_mskc, 4 * j)
                post_turn(j)
                hidden(j, 1, slot)
                expert_mask(j, 0)
                outputs(j, 0)
                hidden(j, 2, slot)
                expert_mask(j, 1)
                outputs(j, 1)
                if last:
                    queue_bases()
                expert_mask(j, 2)
                hidden(j, 3, slot)
                outputs(j, 2)
                expert_mask(j, 3)
                if last_post:
                    post_cols(NB - 1)
                outputs(j, 3)
                if last_post:
                    post_gate(NB - 1)
                if last:
                    pe.wait_ge(s_cntc, 1)
                    rows_back(NB - 1)

            pe.wait_ge(s_khl, 2 * NB)
            pe.wait_ge(zeroed, 5)
            attention(0, True)
            attention(1, False, second=False)
            pe.wait_ge(ld_w2, 32)
            pe.wait_ge(s_wcut, 3)
            experts(0)
            with pe.Fori(2, NB - 1) as j:
                attention(j, False)
                experts(j - 1)
            attention(NB - 1, False)
            experts(NB - 2, last_post=True)
            experts(NB - 1, slot=1)

        @block.vector
        def _(dve):
            V = nc.vector

            class Steps:

                def __init__(self, s, base=0):
                    self.s, self.base, self.n = s, base, 0

                def __call__(self, ins):
                    self.n += 1
                    ins.then_inc(self.s, 1)
                    dve.wait_ge(self.s, add(self.base, self.n))

            step = Steps(dv)

            def bc(ap, n=D):
                return ap.unsqueeze(ap.ndim).broadcast_to([*ap.shape, n])

            def rows(v, n):
                return v.unsqueeze(1).broadcast_to([ROWS, n, v.shape[-1]])

            dve.sem_inc(s_part, 2)

            def inverse_root(x, y, t):
                step(V.tensor_scalar(t.bitcast(I32), x.bitcast(I32), 1, None, ALU.logical_shift_right))
                step(V.tensor_scalar(y.bitcast(I32), t.bitcast(I32), -1.0, float(0x5F3759DF), ALU.mult, ALU.add))
                for _ in range(3):
                    step(V.scalar_tensor_tensor(t, y, -0.5, y, ALU.mult, ALU.mult))
                    step(V.tensor_tensor(t, t, x, ALU.mult))
                    step(V.scalar_tensor_tensor(y, t, 1.5, y, ALU.add, ALU.mult))

            dve.wait_ge(ld_pack, 16)
            g1, g2 = packed_at("g1", HALF), packed_at("g2")
            for c in range(2):
                step(V.tensor_scalar(w1g[:, c], w1t[:, c, 0], g1[:, c:c + 1], None, ALU.mult))
            step(V.tensor_reduce(cen[0:HALF, 0:2], w1g[:], AX.X, ALU.add))
            step(V.tensor_scalar(cen[0:HALF, 2:4], cen[0:HALF, 0:2], 1.0 / D, None, ALU.mult))
            for c in range(2):
                step(V.tensor_scalar(w1g[:, c], w1g[:, c], cen[0:HALF, 2 + c:3 + c], None, ALU.subtract))
            step(V.tensor_scalar(wp1g[:], packed_at("wp1"), g2, None, ALU.mult))
            step(V.tensor_reduce(cen[:, 4:5], wp1g[:], AX.X, ALU.add))
            step(V.tensor_scalar(cen[:, 5:6], cen[:, 4:5], 1.0 / D, None, ALU.mult))
            dve.wait_ge(zeroed, 3)
            for half in range(2):
                r = slice(half * D, (half + 1) * D)
                step(V.tensor_scalar(wp1d[r, half], wp1g[r], cen[r, 5:6], None, ALU.subtract))
            dve.sem_inc(s_wts, 1)
            dve.wait_ge(s_bias, 1)
            step(V.tensor_tensor(b1c[:, 0:1], pR[:, 3, 64:65], packed_at("b1"), ALU.add))
            step(V.tensor_tensor(bias2[:], pR[0:ROWS, 3, 128:128 + D], packed_at("bp1", ROWS), ALU.add))
            dve.sem_inc(s_b1, 1)
            step(V.tensor_reduce(cen[0:ROWS, 6:7], bias2[:], AX.X, ALU.add))
            step(V.tensor_scalar(cen[0:ROWS, 7:8], cen[0:ROWS, 6:7], 1.0 / D, None, ALU.mult))
            step(V.tensor_scalar(bias2[:], bias2[:], cen[0:ROWS, 7:8], None, ALU.subtract))
            dve.wait_ge(s_b1c, 1)
            step(V.tensor_copy(b1c[:, 1:2], pR[:, 3, 65:66]))
            dve.sem_inc(s_biasc, 1)
            V.memset(ones_run[:], 1.0)

            def first_norm(w0, w1_):
                for w in range(w0, w1_):
                    i = V.bn_stats(stats[:, w], img[:, :, w, :])
                step(i)
                me, mo, ve, vo = (stats[:, w0:w1_, k] for k in (1, 4, 2, 5))
                var, r, t, dif, dif2, vsum, mu = (small[:, k, w0:w1_] for k in (0, 1, 11, 8, 9, 10, 7))
                step(V.tensor_tensor(dif, me, mo, ALU.subtract))
                step(V.tensor_tensor(t, me, mo, ALU.add))
                step(V.tensor_tensor(dif2, dif, dif, ALU.mult))
                step(V.tensor_tensor(vsum, ve, vo, ALU.add))
                step(V.tensor_scalar(dif2, dif2, 0.25, EPS, ALU.mult, ALU.add))
                step(V.scalar_tensor_tensor(var, vsum, 1.0 / PD, dif2, ALU.mult, ALU.add))
                step(V.tensor_scalar(mu, t, 0.5, None, ALU.mult))
                inverse_root(var, r, t)
                V.scalar_tensor_tensor(small[:, 6, w0:w1_], mu, -1.0, r, ALU.mult, ALU.mult).then_inc(s_ln1, 1)
                for w in range(w0, w1_):
                    if w % GW in ACT_WP:
                        continue
                    i = V.tensor_scalar(xn[:, w].rearrange("p (a r) -> p a r", r=PATCH), img[:, :, w, :],
                                        small[:, 7, w:w + 1], small[:, 1, w:w + 1], ALU.subtract, ALU.mult)
                    if w % GW == DVE_LAST:
                        i.then_inc(s_xn, 1)

            dve.wait_ge(ld_img, CH * B * 16)
            first_norm(0, 4 * GW)
            first_norm(4 * GW, W)

            def wps(group):
                return slice(group[0] * GW, (group[-1] + 1) * GW)

            def token_roots(n):
                q = wps(GROUPS[n])
                dve.wait_ge(s_ssq, GROUPS[n][-1] + 1)
                step(V.tensor_scalar(small[:, 2, q], pR[0:ROWS, SUM_BANK[n], q], 1.0 / D, EPS, ALU.mult, ALU.add))
                inverse_root(small[:, 2, q], small[:, 3, q], small[:, 11, q])

            def take_second(k):
                p = PAIRS[k]
                dve.wait_ge(s_mm1, k // 2 + 1)
                u = pS[0:ROWS, k % 2, 0:(p.stop - p.start) * D].rearrange("p (w d) -> p w d", d=D)
                step(V.tensor_tensor(tc[:, p], u, bc(small[:, 3, p]), ALU.mult))
                V.tensor_tensor(ta[:, p], tc[:, p], rows(bias2[:], p.stop - p.start), ALU.add).then_inc(s_p, 1)

            def third_sums(n):
                q = wps(GROUPS[n])
                for k in (2 * n, 2 * n + 1):
                    dve.wait_ge(s_sq, k + 1)
                    i = V.tensor_reduce(small[:, 9, PAIRS[k]], tb[:, PAIRS[k]], AX.X, ALU.add)
                step(i)
                step(V.tensor_scalar(small[:, 4, q], small[:, 9, q], 1.0 / D, EPS, ALU.mult, ALU.add))

            def third_norm(n, y):
                for k in (2 * n, 2 * n + 1):
                    V.tensor_tensor(tc[:, PAIRS[k]], ta[:, PAIRS[k]], bc(small[:, y, PAIRS[k]]),
                                    ALU.mult).then_inc(s_z, 1)

            def expert_scale():
                dve.wait_ge(s_wmax, 1)
                step(V.tensor_scalar(wmax[:, 2:3], wmax[:, 1:2], 1e-30, None, ALU.max))
                step(V.tensor_scalar(wmax[:, 3:4].bitcast(I32), wmax[:, 2:3].bitcast(I32), 0x7F800000, None,
                                     ALU.bitwise_and))
                step(V.reciprocal(wmax[:, 5:6], wmax[:, 3:4]))
                step(V.tensor_scalar(wmax[:, 4:5], wmax[:, 5:6], WTOP, None, ALU.mult))
                step(V.tensor_scalar(wmax[:, 6:7], wmax[:, 3:4], 1.0 / (WTOP * SPLIT), None, ALU.mult))
                step(V.tensor_scalar(eb1s[:], packed_at("eb1"), wmax[:, 4:5], SPLIT, ALU.mult, ALU.mult))
                step(V.tensor_scalar(b2s[:], packed_at("b2"), wmax[:, 4:5], SPLIT, ALU.mult, ALU.mult))
                dve.sem_inc(s_wscale, 1)

            def silu(g):
                dve.wait_ge(s_zc, 2 * (g + 1))
                if g >= 2:
                    dve.wait_ge(s_mm2, g - 1)
                V.scalar_tensor_tensor(sc[:, g % 2], th[:, g % 2], 1.0, zc[:, g % 2], ALU.add, ALU.mult).then_inc(s_sc, 1)

            def take_h(g):
                dve.wait_ge(s_mm2, g + 1)
                u = pR[0:ROWS, H_BANK[g], 0:GW * D].rearrange("p (w d) -> p w d", d=D)
                V.tensor_tensor(h_all[:, g * GW:(g + 1) * GW], u, rows(packed_at("bp2", ROWS), GW), ALU.add).then_inc(s_h, 1)

            def h_sums(n, x):
                q = wps(GROUPS[n])
                dve.wait_ge(s_hsq, GROUPS[n][-1] + 1)
                step(V.tensor_reduce(small[:, 9, q], tb[:, q], AX.X, ALU.add))
                step(V.tensor_scalar(small[:, x, q], small[:, 9, q], 1e-30, None, ALU.max))

            def h_scale(n, y):
                q = wps(GROUPS[n])
                step(V.tensor_scalar(small[:, 10, q], small[:, y, q], 1.0 / NORM_EPS, SPLIT, ALU.min, ALU.mult))
                dve.wait_ge(s_h, GROUPS[n][-1] + 1)

            def unit_vectors(g):
                q = slice(g * GW, (g + 1) * GW)
                V.tensor_tensor(f_all[:, q], h_all[:, q], bc(small[:, 10, q]), ALU.mult).then_inc(s_f, 1)

            def split_f(g):
                q = slice(g * BLK, (g + 1) * BLK)
                dve.wait_ge(s_ftc, 2 * (g + 1))
                V.tensor_tensor(QL[:, q], pS[:, F_BANK[g], 0:BLK], QH[:, q], ALU.subtract).then_inc(s_ql, 1)
                V.tensor_copy(KHL[0:D, q], QH[0:D, q]).then_inc(s_khl, 1)
                dve.wait_ge(s_ql, g + 1)
                V.tensor_copy(KHL[D:D2, q], QL[D:D2, q]).then_inc(s_khl, 1)

            token_roots(0)
            take_second(0)
            take_second(1)
            third_sums(0)
            q = wps(GROUPS[0])
            inverse_root(small[:, 4, q], small[:, 5, q], small[:, 11, q])
            third_norm(0, 5)
            token_roots(1)
            silu(0)
            take_second(2)
            silu(1)
            take_h(0)
            take_second(3)
            silu(2)
            take_h(1)
            silu(3)
            take_h(2)
            take_h(3)
            third_sums(1)
            h_sums(0, 5)
            flat = small[:].rearrange("p k w -> p (k w)")
            first = len(GROUPS[0]) * GW
            inverse_root(flat[:, 4 * W + first:5 * W + first], flat[:, 8 * W + first:9 * W + first], small[:, 11])
            third_norm(1, 8)
            h_scale(0, 9)
            unit_vectors(0)
            unit_vectors(1)
            silu(4)
            silu(5)
            take_h(4)
            unit_vectors(2)
            unit_vectors(3)
            silu(6)
            take_h(5)
            take_h(6)
            h_sums(1, 6)
            q = wps(GROUPS[1])
            inverse_root(small[:, 6, q], small[:, 8, q], small[:, 11, q])
            h_scale(1, 8)
            for g in GROUPS[1]:
                unit_vectors(g)
            for g in range(NB):
                split_f(g)
            dve.wait_ge(ld_w1, 32)
            V.tensor_reduce(wmax[:, 0:1], ew1[:].rearrange("p e f -> p (e f)"), AX.X, ALU.max,
                            apply_absolute_value=True).then_inc(s_wmax_in, 1)
            expert_scale()

            NPOST = 22

            def post_steps(j, at):
                s = Steps(dvp, j * NPOST)
                s.n = at
                return s

            def post_blend(j, s):
                dve.wait_ge(s_pnum, add(j, 1))
                s(V.reciprocal(ps_small[:, 0], pDen))
                s(V.tensor_scalar(ps_small[:, 0], ps_small[:, 0], 0.2, None, ALU.mult))
                s(V.tensor_tensor(pt[:, 0], pA, bc(ps_small[:, 0]), ALU.mult))
                s(V.scalar_tensor_tensor(pt[:, 1], f_all[:, bass.ds(j * GW, GW)], 0.8, pt[:, 0], ALU.mult, ALU.add))
                dve.sem_inc(s_pt, 1)

            def post_length(j):
                dve.wait_ge(s_psq, add(j * 2, 1))
                V.tensor_reduce(ps_small[:, 1], pt[:, 3], AX.X, ALU.add).then_inc(s_proot_in, 1)

            def post_center(j, s):
                dve.wait_ge(s_proot, add(j * 2, 1))
                s(V.tensor_scalar(ps_small[:, 3], ps_small[:, 2], 1.0 / (NORM_EPS * SPLIT), None, ALU.min))
                s(V.tensor_tensor(pt[:, 0], pt[:, 1], bc(ps_small[:, 3]), ALU.mult))
                s(V.tensor_tensor(pt[:, 1], pt[:, 0], h_all[:, bass.ds(j * GW, GW)], ALU.add))
                s(V.tensor_reduce(ps_small[:, 6], pt[:, 1], AX.X, ALU.add))
                s(V.scalar_tensor_tensor(pt[:, 2], bc(ps_small[:, 6]), -1.0 / D, pt[:, 1], ALU.mult, ALU.add))
                dve.sem_inc(s_pt, 1)

            def post_variance(j, s):
                dve.wait_ge(s_psq, add(j * 2, 2))
                s(V.tensor_reduce(ps_small[:, 7], pt[:, 3], AX.X, ALU.add))
                V.tensor_scalar(ps_small[:, 4], ps_small[:, 7], 1.0 / D, EPS, ALU.mult, ALU.add).then_inc(s_proot_in, 1)

            def square_here(s, k):
                s(V.tensor_tensor(pt[:, 3], pt[:, k], pt[:, k], ALU.mult))
                dve.sem_inc(s_psq, 1)

            def post_split(j, s, slot):
                dve.wait_ge(s_xh, add(j * 2, 2))
                s(V.scalar_tensor_tensor(xhl[D:D2, slot], xcol[D:D2], SPLIT, xhl[D:D2, slot],
                                         ALU.mult, ALU.subtract))
                dve.sem_inc(s_x16, 1)

            def post_route(j, s):
                blk = bass.ds(j * GW, GW)
                dve.wait_ge(s_log, add(j, 1))
                s(V.tensor_tensor(lg[:, 0], pLog, rows(packed_at("gate_b", ROWS), GW), ALU.add))
                s(V.tensor_reduce(ps_small[:, 8], lg[:, 0], AX.X, ALU.max))
                s(V.tensor_tensor(lg[:, 2], lg[:, 0], bc(ps_small[:, 8], E), ALU.subtract))
                dve.sem_inc(s_lm, 1)
                s(V.tensor_tensor(lg[:, 1], lg[:, 0], bc(ps_small[:, 8], E), ALU.is_ge))
                s(V.tensor_tensor(lg[:, 0], lg[:, 1], rows(packed_at("ramp", ROWS), GW), ALU.mult))
                s(V.tensor_reduce(ps_small[:, 9], lg[:, 0], AX.X, ALU.max))
                s(V.tensor_tensor(hot[:], lg[:, 0], bc(ps_small[:, 9], E), ALU.is_equal))
                dve.sem_inc(s_hot, 1)
                s(V.tensor_copy(oh_all[:, blk], hot[:]))

            def post_weight(j, s):
                dve.wait_ge(s_pe, add(j, 1))
                s(V.tensor_reduce(ps_small[:, 10], lg[:, 3], AX.X, ALU.add))
                s(V.reciprocal(ps_small[:, 11], ps_small[:, 10]))
                s(V.tensor_scalar(weight[:], ps_small[:, 11], wmax[0:ROWS, 6:7], None, ALU.mult))
                assert s.n in (NPOST, NPOST + 2)

            def take_rows(j):
                dve.wait_ge(s_yb, add(j, 1))
                V.tensor_tensor(y_row, pA, bc(weight[:]), ALU.mult).then_inc(s_y, 1)

            def sums(j, first, second=True):
                for p in range(NPAIR):
                    dve.wait_ge(s_exp, add(j * NPAIR, p + 1))
                    if p == 0:
                        if not first:
                            dve.wait_ge(s_pnum, j)
                        i = V.tensor_copy(esum[:], ex[:, 0])
                    else:
                        dve.wait_ge(s_es, add(j * NPAIR, p))
                        if p < LAST:
                            i = V.tensor_tensor(esum[:], esum[:], ex[:, p % NE], ALU.add)
                        else:
                            i = V.tensor_tensor(esum[0:KT_REST, 0], esum[0:KT_REST, 0],
                                                ex[0:KT_REST, p % NE, 0], ALU.add)
                    i.then_inc(s_es, 1)
                    if not first:
                        if p == 0:
                            s = post_steps(j - 1, 0)
                            post_blend(j - 1, s)
                        if p == 1:
                            post_length(j - 1)
                        if p == 2:
                            post_center(j - 1, s)
                        if p == 4:
                            post_variance(j - 1, s)
                        if p == 6 and second:
                            take_rows(j - 2)
                        if p == 10:
                            post_split(j - 1, s, 0)
                if not first:
                    post_route(j - 1, s)
                dve.wait_ge(s_es, add(j * NPAIR, NPAIR))
                V.tensor_tensor(esum[:, 0], esum[:, 0], esum[:, 1], ALU.add).then_inc(s_den, 1)
                return s if not first else None

            NFIN = 13
            NCOMBINE = 6

            def combine(j, p, f):
                dve.wait_ge(s_l2, add(j * 4, p + 3))
                dve.wait_ge(s_mskc, add(j * 4, p + 1))
                o = yacc if p == 0 else ynew
                i = V.scalar_tensor_tensor(o[:], pY[p % 2], b2s[:, p:p + 1], msk[:, p], ALU.add, ALU.mult)
                if p:
                    f(i)
                    i = V.tensor_tensor(yacc[:], yacc[:], ynew[:], ALU.add)
                if p < 3:
                    f(i)
                    dve.sem_inc(s_part, 1)
                else:
                    i.then_inc(s_part, 1)

            def last_norm(s, src, k):
                s(V.tensor_reduce(fin_small[:, 6], src, AX.X, ALU.add))
                s(V.scalar_tensor_tensor(fin_t[:, k], bc(fin_small[:, 6]), -1.0 / D, src, ALU.mult, ALU.add))
                s(V.tensor_tensor(fin_t[:, 3], fin_t[:, k], fin_t[:, k], ALU.mult))
                s(V.tensor_reduce(fin_small[:, 7], fin_t[:, 3], AX.X, ALU.add))
                return V.tensor_scalar(fin_small[:, k], fin_small[:, 7], 1.0 / D, EPS, ALU.mult, ALU.add)

            def finish_kept(j, s, second=False):
                dve.wait_ge(s_ysum, add(j, 1))
                s(V.tensor_tensor(fin_t[:, 2].bitcast(I32), y_row.bitcast(I32), mask[:], ALU.bitwise_and))
                s(V.tensor_tensor(fin_t[:, 2], fin_t[:, 2], rest[:, 2], ALU.add))
                end_half(last_norm(s, fin_t[:, 2], 0), s, second)

            def finish_dropped(j, s, second=True):
                end_half(last_norm(s, h2_all[:, bass.ds(j * GW, GW)], 1), s, second)

            def end_half(ins, s, second):
                if second:
                    ins.then_inc(s_froot_in, 1)
                else:
                    s(ins)

            def finish(j, s):
                blk = bass.ds(j * GW, GW)
                dve.wait_ge(s_froot, add(j, 1))
                s(V.tensor_tensor(ok_all[:, blk], fin_t[:, 0], bc(fin_small[:, 2]), ALU.mult))
                s(V.tensor_tensor(od_all[:, blk], fin_t[:, 1], bc(fin_small[:, 3]), ALU.mult))
                assert s.n == NFIN


            sums(0, True)
            s = sums(1, False, second=False)
            post_weight(0, s)
            c = Steps(dvc)
            for p in range(4):
                combine(0, p, c)
            with dve.Fori(2, NB - 1) as j:
                s = sums(j, False)
                post_weight(j - 1, s)
                c = Steps(dvc, (j - 1) * NCOMBINE)
                combine(j - 1, 0, c)
                f = Steps(dvf, (j - 2) * NFIN)
                finish_kept(j - 2, f)
                combine(j - 1, 1, c)
                finish_dropped(j - 2, f)
                combine(j - 1, 2, c)
                finish(j - 2, f)
                combine(j - 1, 3, c)
            last = NB - 1
            s = sums(last, False)
            c = Steps(dvc, (last - 1) * NCOMBINE)
            post_weight(last - 1, s)
            s = post_steps(last, 0)
            post_blend(last, s)
            square_here(s, 1)
            post_length(last)
            combine(last - 1, 0, c)
            post_center(last, s)
            square_here(s, 2)
            post_variance(last, s)
            combine(last - 1, 1, c)
            combine(last - 1, 2, c)
            post_split(last, s, 1)
            combine(last - 1, 3, c)
            post_route(last, s)
            f = Steps(dvf, (last - 2) * NFIN)
            finish_kept(last - 2, f)
            take_rows(last - 1)
            post_weight(last, s)
            adds = Steps(dvc, last * NCOMBINE)
            combine(last, 0, adds)

            step(V.tensor_copy(ohe[:], oh_all[:].rearrange("p w e -> p e w")))
            step(V.tensor_reduce(rk_small[:, 0], ohe[:], AX.X, ALU.add))
            dve.sem_inc(s_cnt_in, 1)
            step(V.tensor_tensor_scan(pre[:].rearrange("p e w -> p (e w)"), ones_run[:],
                                      ohe[:].rearrange("p e w -> p (e w)"), 0.0, ALU.mult, ALU.add))
            combine(last, 1, adds)
            finish_dropped(last - 2, f)
            dve.wait_ge(s_cnt, 1)
            step(V.tensor_copy(rk_small[:, 1:3].rearrange("p a e -> p (a e)"), pM[0:ROWS, 0:2 * E]))
            dve.sem_inc(s_cntc, 1)
            step(V.tensor_tensor(rk_small[:, 1, 1:E], rk_small[:, 1, 1:E], pre[:, 0:E - 1, W - 1], ALU.subtract))
            step(V.tensor_tensor(rk[:, 0], pre[:].rearrange("p e w -> p w e"), rows(rk_small[:, 1], W), ALU.add))
            step(V.tensor_tensor(rk[:, 1], rk[:, 0], oh_all[:], ALU.mult))
            step(V.tensor_reduce(rkw[:, 0], rk[:, 1], AX.X, ALU.add))
            step(V.tensor_tensor(rk[:, 2], oh_all[:], rows(rk_small[:, 2], W), ALU.mult))
            step(V.tensor_reduce(rkw[:, 1], rk[:, 2], AX.X, ALU.add))
            for c in range(COPIES):
                step(V.scalar_tensor_tensor(rkw[:, 2], rkw[:, 1], float(c), rkw[:, 0], ALU.mult, ALU.add))
                step(V.tensor_scalar(kept[:, c], rkw[:, 2], float(CAP), None, ALU.is_le))

            def choose(n, c, q):
                dve.wait_ge(s_oc, n * COPIES + c + 1)
                V.copy_predicated(o_all[:, c, q], bc(kept[:, c, q].bitcast(U32)), ok_all[:, q]).then_inc(s_out, 1)

            finish(last - 2, f)
            dve.sem_inc(s_od, 1)
            f = Steps(dvf, (last - 1) * NFIN)
            finish_kept(last - 1, f)
            finish_dropped(last - 1, f)
            combine(last, 2, adds)
            combine(last, 3, adds)
            take_rows(last)
            choose(0, 0, PARTS[0])
            finish(last - 1, f)
            choose(0, 1, PARTS[0])
            choose(0, 2, PARTS[0])
            f = Steps(dvf, last * NFIN)
            finish_dropped(last, f, second=False)
            finish_kept(last, f, second=True)
            finish(last, f)
            dve.sem_inc(s_od, 1)
            for c in range(COPIES):
                choose(1, c, PARTS[1])


def kernel(**inputs):
    import concourse.bacc as bacc
    from concourse.bass_utils import run_bass_kernel_spmd as run

    nc = bacc.Bacc("TRN2", target_bir_lowering=False, num_devices=1)
    arrays = {"in_packed": pack(inputs), "in_select": selectors()}
    arrays.update({f"in_{n}": np.ascontiguousarray(inputs[n]) for n in ("x", "L0_ffn_w1", "L0_ffn_w2")})
    args = [nc.dram_tensor(n, a.shape, mybir.dt.from_np(a.dtype), kind="ExternalInput").ap()
            for n, a in arrays.items()]
    out = nc.dram_tensor("out_h", (B, COPIES * HP * W, D), F32, kind="ExternalOutput").ap()
    vit_layer(nc, *args, out)
    r = run(nc, [arrays], core_ids=[0])
    return r.results[0]["out_h"]
```
